# Optimizing a Trainium2 kernel written in Bass

```python
import numpy as np
import jax
import jax.numpy as jnp

def _softmax(x, axis=-1):
    return jax.nn.softmax(x, axis=axis)

def _gelu(x):
    return jax.nn.gelu(x, approximate=True)

def _silu(x):
    return jax.nn.silu(x)

def _sigmoid(x):
    return jax.nn.sigmoid(x)

def _layernorm(x, axis=-1, eps=1e-05):
    m = jnp.mean(x, axis=axis, keepdims=True)
    v = jnp.var(x, axis=axis, keepdims=True)
    return (x - m) / jnp.sqrt(v + eps)

def _scatter_add(tgt, idx, src, axis=0):
    return tgt.at[idx].add(src)

def _segment_sum(src, seg, n):
    return jax.ops.segment_sum(src, seg, n)
kernel_name = 'mk_cond_seq_d1_seqx_r4_a2fa7e'

def setup_inputs(seed: int=0):
    np.random.seed(seed)
    _w = jnp.asarray

    def _rec_inputs():
        import jax
        import jax.numpy as jnp
        _rk = jax.random.key(seed)
        x = -0.0002928 + 1 * jax.random.normal(jax.random.fold_in(_rk, 1), (2, 1024, 256), jnp.float32)
        _lenS = 1024 - jax.random.randint(jax.random.fold_in(_rk, 7), (2,), 0, max(1, 1024 // 4) + 1, jnp.int32)
        _lenS2 = 1024 - jax.random.randint(jax.random.fold_in(_rk, 8), (2,), 0, max(1, 1024 // 4) + 1, jnp.int32)
        cond_1024 = 0.0061147 + 1.02565 * jax.random.normal(jax.random.fold_in(_rk, 11), (2, 256), jnp.float32)
        _validS = jnp.arange(1024)[None, :] < _lenS[:, None]
        _validS2 = jnp.arange(1024)[None, :] < _lenS2[:, None]
        _causal = jnp.tril(jnp.ones((1024, 1024), dtype=bool))
        mask_BxS_bk0 = jnp.logical_not(jnp.broadcast_to(_validS[:, :], (2, 1024)))
        return (x, cond_1024, mask_BxS_bk0)
    x, cond_1024, mask_BxS_bk0 = _rec_inputs()

    def _L0_cond_setup():
        import jax, jax.numpy as jnp
        import numpy as np
        B, N, C = (4, 256, 256)
        H = 16
        D = C // H
        FF = 4 * C
        EPS = 1e-05

        def _layernorm(x):
            mu = jnp.mean(x, axis=-1, keepdims=True)
            var = jnp.mean(jnp.square(x - mu), axis=-1, keepdims=True)
            return (x - mu) * jax.lax.rsqrt(var + EPS)

        def _modulate(x, shift, scale):
            return x * (1.0 + scale[:, None, :]) + shift[:, None, :]

        def _attention(x, node_mask, qkv_w, proj_w, proj_b):
            b, n, c = x.shape
            qkv = (x @ qkv_w).reshape(b, n, 3, H, D)
            q, k, v = jnp.moveaxis(qkv, 2, 0)
            q = q.transpose(0, 2, 1, 3)
            k = k.transpose(0, 2, 1, 3)
            v = v.transpose(0, 2, 1, 3)
            scale = D ** (-0.5)
            scores = jnp.einsum('bhnd,bhmd->bhnm', q, k) * scale
            mask = node_mask[:, None, None, :]
            scores = jnp.where(mask, scores, -jnp.inf)
            attn = jax.nn.softmax(scores, axis=-1)
            out = jnp.einsum('bhnm,bhmd->bhnd', attn, v)
            out = out.transpose(0, 2, 1, 3).reshape(b, n, c)
            return out @ proj_w + proj_b

        def _mlp(x, fc1_w, fc1_b, fc2_w, fc2_b):
            h = jax.nn.gelu(x @ fc1_w + fc1_b, approximate=False)
            return h @ fc2_w + fc2_b
        key = jax.random.key(seed)
        ks = jax.random.split(key, 16)
        s = 0.02
        return {'x': jax.random.normal(ks[0], (B, N, C), jnp.float32), 'c': jax.random.normal(ks[1], (B, C), jnp.float32), 'node_mask': jax.random.randint(ks[2], (B, N), 0, 2) > 0, 'qkv_w': jax.random.normal(ks[3], (C, 3 * C), jnp.float32) * s, 'proj_w': jax.random.normal(ks[4], (C, C), jnp.float32) * s, 'proj_b': jnp.zeros((C,), jnp.float32), 'fc1_w': jax.random.normal(ks[5], (C, FF), jnp.float32) * s, 'fc1_b': jnp.zeros((FF,), jnp.float32), 'fc2_w': jax.random.normal(ks[6], (FF, C), jnp.float32) * s, 'fc2_b': jnp.zeros((C,), jnp.float32), 'ada1_w': jax.random.normal(ks[7], (C, C), jnp.float32) * s, 'ada1_b': jnp.zeros((C,), jnp.float32), 'ada2_w': jax.random.normal(ks[8], (C, 6 * C), jnp.float32) * s, 'ada2_b': jnp.zeros((6 * C,), jnp.float32)}
    _L0_cond_all = _L0_cond_setup()
    _L0_cond_in = {k: v for k, v in _L0_cond_all.items() if k in ('qkv_w', 'proj_w', 'proj_b', 'fc1_w', 'fc1_b', 'fc2_w', 'fc2_b', 'ada1_w', 'ada1_b', 'ada2_w', 'ada2_b')}
    del _L0_cond_all
    return {'x': x, 'cond_1024': cond_1024, 'mask_BxS_bk0': mask_BxS_bk0, 'L0_cond_qkv_w': _L0_cond_in['qkv_w'], 'L0_cond_proj_w': _L0_cond_in['proj_w'], 'L0_cond_proj_b': _L0_cond_in['proj_b'], 'L0_cond_fc1_w': _L0_cond_in['fc1_w'], 'L0_cond_fc1_b': _L0_cond_in['fc1_b'], 'L0_cond_fc2_w': _L0_cond_in['fc2_w'], 'L0_cond_fc2_b': _L0_cond_in['fc2_b'], 'L0_cond_ada1_w': _L0_cond_in['ada1_w'], 'L0_cond_ada1_b': _L0_cond_in['ada1_b'], 'L0_cond_ada2_w': _L0_cond_in['ada2_w'], 'L0_cond_ada2_b': _L0_cond_in['ada2_b']}

def reference(x, cond_1024, mask_BxS_bk0, L0_cond_qkv_w, L0_cond_proj_w, L0_cond_proj_b, L0_cond_fc1_w, L0_cond_fc1_b, L0_cond_fc2_w, L0_cond_fc2_b, L0_cond_ada1_w, L0_cond_ada1_b, L0_cond_ada2_w, L0_cond_ada2_b):
    import jax
    import jax.numpy as jnp

    def _L0_cond_ref(x, c, node_mask, qkv_w, proj_w, proj_b, fc1_w, fc1_b, fc2_w, fc2_b, ada1_w, ada1_b, ada2_w, ada2_b):
        import jax, jax.numpy as jnp
        import numpy as np
        B, N, C = (4, 256, 256)
        H = 16
        D = C // H
        FF = 4 * C
        EPS = 1e-05

        def _layernorm(x):
            mu = jnp.mean(x, axis=-1, keepdims=True)
            var = jnp.mean(jnp.square(x - mu), axis=-1, keepdims=True)
            return (x - mu) * jax.lax.rsqrt(var + EPS)

        def _modulate(x, shift, scale):
            return x * (1.0 + scale[:, None, :]) + shift[:, None, :]

        def _attention(x, node_mask, qkv_w, proj_w, proj_b):
            b, n, c = x.shape
            qkv = (x @ qkv_w).reshape(b, n, 3, H, D)
            q, k, v = jnp.moveaxis(qkv, 2, 0)
            q = q.transpose(0, 2, 1, 3)
            k = k.transpose(0, 2, 1, 3)
            v = v.transpose(0, 2, 1, 3)
            scale = D ** (-0.5)
            scores = jnp.einsum('bhnd,bhmd->bhnm', q, k) * scale
            mask = node_mask[:, None, None, :]
            scores = jnp.where(mask, scores, -jnp.inf)
            attn = jax.nn.softmax(scores, axis=-1)
            out = jnp.einsum('bhnm,bhmd->bhnd', attn, v)
            out = out.transpose(0, 2, 1, 3).reshape(b, n, c)
            return out @ proj_w + proj_b

        def _mlp(x, fc1_w, fc1_b, fc2_w, fc2_b):
            h = jax.nn.gelu(x @ fc1_w + fc1_b, approximate=False)
            return h @ fc2_w + fc2_b
        ada = jax.nn.silu(c @ ada1_w + ada1_b) @ ada2_w + ada2_b
        shift_msa, scale_msa, gate_msa, shift_mlp, scale_mlp, gate_mlp = jnp.split(ada, 6, axis=1)
        attn_out = _attention(x, node_mask, qkv_w, proj_w, proj_b)
        x = x + gate_msa[:, None, :] * _modulate(_layernorm(attn_out), shift_msa, scale_msa)
        mlp_out = _mlp(x, fc1_w, fc1_b, fc2_w, fc2_b)
        x = x + gate_mlp[:, None, :] * _modulate(_layernorm(mlp_out), shift_mlp, scale_mlp)
        return x
    x = _L0_cond_ref(x, cond_1024, mask_BxS_bk0, L0_cond_qkv_w, L0_cond_proj_w, L0_cond_proj_b, L0_cond_fc1_w, L0_cond_fc1_b, L0_cond_fc2_w, L0_cond_fc2_b, L0_cond_ada1_w, L0_cond_ada1_b, L0_cond_ada2_w, L0_cond_ada2_b)
    return x

_drawn_inputs = setup_inputs


def setup_inputs(seed=0):
    import zlib

    import numpy as np

    out = dict(_drawn_inputs(seed))
    spreads = {'L0_cond_proj_b': (0.0, 0.1),
     'L0_cond_fc1_b': (0.0, 0.28),
     'L0_cond_fc2_b': (0.0, 0.1),
     'L0_cond_ada1_b': (0.0, 0.319),
     'L0_cond_ada2_b': (0.0, 0.1)}
    factors = {}
    for name, (base, spread) in spreads.items():
        noise = np.random.default_rng([zlib.crc32(name.encode()), seed]).standard_normal(out[name].shape)
        drawn = base * np.exp(spread * noise) if base else spread * noise
        out[name] = jnp.asarray(drawn.astype(out[name].dtype))
    for name, factor in factors.items():
        out[name] = (out[name] * factor).astype(out[name].dtype)
    return out
```

```python
from contextlib import ExitStack

import numpy as np

import concourse.bass as bass
from concourse import mybir

F32 = mybir.dt.float32
BF16 = mybir.dt.bfloat16
I32 = mybir.dt.int32
U8 = mybir.dt.uint8
ALU = mybir.AluOpType
ACT = mybir.ActivationFunctionType
AX = mybir.AxisListType

NB, S, C, H = 2, 1024, 256, 16
D = C // H
FF = 4 * C
EPS = 1e-5
P = 128
KC = C // P
HC = P // D
T = NB * S
BLK = 512
KB = 256
NKB = S // KB
KEYS_FAST = KB
KT = KB // P
UNITS = NB * H // 4
QT = S // P
CHUNKS = 8
ROWS = 100
ONE_ROW, MAX_ROW = 96, 97
MASKED = 1.0e30
Q_PARTS = (0, 1, 2, 0, 1, 0)
K_PARTS = (0, 0, 0, 1, 1, 2)


def cond_block(nc, xT, x, cT, mask, mask_cols, ident, wqkv, wp, bp, w1, b1, w2, b2, wa1, ba1, wa2, ba2, out):
    ot_dram = nc.dram_tensor("attention_rows", (UNITS, P, S), F32, kind="Internal").ap()
    with ExitStack() as ctx:
        def sb(name, shape, dt):
            return ctx.enter_context(nc.sbuf_tensor(name, shape, dt))

        def sem(name):
            return ctx.enter_context(nc.semaphore(name))

        def view(region, at, shape, dt=F32):
            size = int(np.prod(shape)) * (1 if dt == F32 else 0.5)
            v = region[:, at:at + int(size)]
            if dt != F32:
                v = v.bitcast(dt)
            names = "abcd"[:len(shape)]
            if len(shape) > 1:
                v = v.rearrange(f"p ({' '.join(names)}) -> p {' '.join(names)}",
                                **{n: s for n, s in zip(names, shape)})
            return v

        r_qst = sb("r_qst", [P, UNITS * 4 * S // 2], F32)
        qst = view(r_qst, 0, [UNITS * 4, S], BF16)
        kst = sb("kst", [P, UNITS * 4, KB], BF16)
        vaug = sb("vaug", [P, UNITS, KT, 4, 2 * D], F32)
        vunit = sb("vunit", [P, 2, KT, 4 * 2 * D], F32)
        r_x = sb("r_x", [P, KC * T], F32)
        xTs = view(r_x, 0, [KC, T])
        probs = view(r_x, 0, [4, 2, BLK])
        r_split = sb("r_split", [P, 5632], F32)
        qsp = view(r_split, 0, [2, 3, S], BF16)
        ksp = view(r_split, 3072, [KC, 3, NB * KB], BF16)
        rest = view(r_split, 4608, [2, BLK])
        numer = view(r_split, 0, [S])
        denom = view(r_split, 1024, [S])
        ots = sb("ots", [P, 2, S], F32)
        r_attn = sb("r_attn", [P, 4608], F32)
        attn = view(r_attn, 0, [4, S])
        wa2s = view(r_attn, 0, [KC, 6 * C])
        ba2s = view(r_attn, 3072, [6 * C])
        wqkvs = sb("wqkvs", [P, KC, 3 * C], F32)
        wps = sb("wps", [P, KC, C], F32)
        w1s = sb("w1s", [P, KC, FF], F32)
        w2s = sb("w2s", [P, FF // P, C], F32)
        wa1s = sb("wa1s", [P, KC, C], F32)
        cTs = sb("cTs", [P, KC, NB], F32)
        b1s = sb("b1s", [P, FF // P], F32)
        ba1s = sb("ba1s", [P, KC], F32)
        bps = sb("bps", [P, C], F32)
        b2s = sb("b2s", [P, C], F32)
        mods = sb("mods", [P, NB, 6, C], F32)
        sil = sb("sil", [P, 3, KC * NB], F32)
        identf = sb("identf", [P, P], F32)
        identb = sb("identb", [P, P], BF16)
        mask8 = sb("mask8", [P, NB * QT], U8)
        maskc = sb("maskc", [P, NB, QT], F32)
        maskb = sb("maskb", [P, NB, KT], F32)
        mrow8 = sb("mrow8", [1, NB, S], U8)
        mbias = sb("mbias", [1, NB, S], BF16)
        ones = sb("ones", [1, S], BF16)
        flagf = sb("flagf", [1, 1], F32)
        flag = sb("flag", [1, 1], I32)
        nmax = sb("nmax", [P, 2, 4, QT], F32)
        nmsp = sb("nmsp", [P, 2, 3, 4 * QT], BF16)
        nmrest = sb("nmrest", [P, 2, 4 * QT], F32)
        nmT = sb("nmT", [96, 2, P], BF16)
        nmall = sb("nmall", [P, UNITS, 4 * QT], F32)
        PS = ctx.enter_context(nc.psum_tensor("PS", [P, 8, BLK], F32))

        hid = [view(r_qst, 4096 * i, [FF // P, BLK]) for i in range(2)]
        x1T = [view(r_qst, 8192 + 1024 * i, [KC, BLK]) for i in range(2)]
        x1 = [view(r_qst, 10240 + 1024 * i, [4, C]) for i in range(2)]
        y1 = view(r_qst, 12288, [4, C])
        y2 = view(r_qst, 13312, [4, C])
        xb = [view(r_qst, 14336 + 1024 * i, [4, C]) for i in range(2)]
        resid = view(r_x, 0, [4, C])
        fin = [view(r_x, 1024 * (1 + i), [4, C]) for i in range(2)]
        stats = sb("stats", [P, 4, 6], F32)
        mv = sb("mv", [P, 2, 4, 2], F32)
        nwt = sb("nwt", [P, 4, 4], F32)

        w_loaded, x_loaded = sem("w_loaded"), [sem(f"x_loaded{i}") for i in range(4)]
        mask_loaded, ada_loaded, mlp_loaded = sem("mask_loaded"), sem("ada_loaded"), sem("mlp_loaded")
        consts = sem("consts")
        rows_set = sem("rows_set")
        rows_dma = sem("rows_dma")
        proj_done, v_done = sem("proj_done"), sem("v_done")
        hi_done = sem("hi_done")
        rest_done, mid_done = sem("rest_done"), sem("mid_done")
        lo_done = sem("lo_done")
        v_evac = sem("v_evac")
        vmask_done = sem("vmask_done")
        q_dma, k_dma = [sem(f"q_dma{i}") for i in range(4)], sem("k_dma")
        q_ready = sem("q_ready")
        ada1_done, ada2_done = sem("ada1_done"), sem("ada2_done")
        sil_exp = sem("sil_exp")
        mods_set = sem("mods_set")
        mx_done, red_done = sem("mx_done"), sem("red_done")
        nm_split, nmT_done = sem("nm_split"), sem("nmT_done")
        nmT_evac, m_dma = sem("nmT_evac"), sem("m_dma")
        st_done, exp_done = sem("st_done"), sem("exp_done")
        pv_done, ot_evac = sem("pv_done"), sem("ot_evac")
        vunit_set = sem("vunit_set")
        ot_dma, nd_dma = [sem("ot_dma0"), sem("ot_dma1")], sem("nd_dma")
        recip_done, attn_ready = sem("recip_done"), sem("attn_ready")
        flag_step = sem("flag_step")
        sp_passed = sem("sp_passed")
        dve_step = sem("dve_step")
        g_x, g_proj, g_hi, g_mid, g_lo, g_kdma = (sem(n) for n in ("g_x", "g_proj", "g_hi", "g_mid", "g_lo", "g_kdma"))
        g_mx, g_red, g_min = (sem(n) for n in ("g_mx", "g_red", "g_min"))
        g_nm, g_nmT, g_nmTe, g_mdma = (sem(n) for n in ("g_nm", "g_nmT", "g_nmTe", "g_mdma"))
        g_rest, g_vm, g_vcol, g_vu, g_zero, g_zdma, g_old = (sem(n) for n in (
            "g_rest", "g_vm", "g_vcol", "g_vu", "g_zero", "g_zdma", "g_old"))
        g_st, g_exp, g_pv, g_add, g_store = (sem(n) for n in ("g_st", "g_exp", "g_pv", "g_add", "g_store"))
        xb_loaded, out_dma = [sem("xb_loaded0"), sem("xb_loaded1")], [sem("out_dma0"), sem("out_dma1")]
        y1_mm, x1T_mm, fc1_mm, fc2_mm = (sem(n) for n in ("y1_mm", "x1T_mm", "fc1_mm", "fc2_mm"))
        y1_set, z1_done, y2_set, z2_done = (sem(n) for n in ("y1_set", "z1_done", "y2_set", "z2_done"))
        x1T_set, gelu_done = sem("x1T_set"), sem("gelu_done")
        xb_set, x1_scaled, x1_done = sem("xb_set"), sem("x1_scaled"), sem("x1_done")
        fin_scaled, resid_set, fin_done = sem("fin_scaled"), sem("resid_set"), sem("fin_done")

        ITEMS = [("q", 0, 0, 0), ("q", 0, 0, 1), ("k", 0), ("k", 1), ("v", 0), ("v", 1), ("q", 0, 1, 0), ("q", 0, 1, 1),
                 ("q", 1, 0, 0), ("q", 1, 0, 1), ("q", 1, 1, 0), ("q", 1, 1, 1)]
        SPLITS = [it for it in ITEMS if it[0] != "v"]
        bank_of = {it: n % 8 for n, it in enumerate(ITEMS)}
        N_Q = len(Q_PARTS) * 16
        G_KDMA = 16 * NB * (KC * len(K_PARTS) + 1)

        def parts_of(item):
            if item[0] == "k":
                return ksp[:, item[1]]
            _, b, c, half = item
            return qsp[:, (2 * b + c) % 2, :, half * BLK:(half + 1) * BLK]

        def slot(u, qt, pair):
            return 2 * QT * u + 2 * qt + pair

        def chunk_of(k):
            return k // 4, k // 2 % 2, k % 2

        block = ctx.enter_context(nc.Block())


        def sp_wait(signal, value):
            nc.sync.wait_ge(signal, value)
            nc.sync.sem_inc(sp_passed, 1)

        def general_sp(sp, xv, k_rows):
            xg = xTs[:, :, 0:NB * KB].rearrange("p k (b t) -> p k b t", b=NB)

            def project(k, kb):
                for b in range(NB):
                    sp.dma_start(xg[:, :, b, :], xv[:, :, b, bass.ds(kb * KB, KB)]).then_inc(g_x, 16)
                sp_wait(g_lo, k + 1)
                for b in range(NB):
                    for c in range(KC):
                        k_rows(b, c, g_kdma)
                    sp.dma_start(kst[ONE_ROW:ONE_ROW + 1, H * b:H * (b + 1), :],
                                 mbias[0:1, b:b + 1, bass.ds(kb * KB, KB)].to_broadcast([1, H, KB])).then_inc(g_kdma, 16)
                sp_wait(g_kdma, G_KDMA * (k + 1))

            with sp.Fori(0, NKB) as kb:
                project(kb, kb)
                sp_wait(g_mx, 2 * QT * UNITS * kb + 2 * QT * UNITS)
            with sp.Fori(0, UNITS) as u:
                sp_wait(g_nmTe, u + 1)
                sp.dma_start(qst[MAX_ROW:ROWS, bass.ds(4 * u, 4), :], nmT[:, 0, :]).then_inc(g_mdma, 16)
                sp_wait(g_mdma, 16 * (u + 1))
            sp.wait_ge(g_zero, 1)
            with sp.Fori(0, UNITS) as u:
                sp.dma_start(ot_dram[bass.ds(u, 1), :, :].rearrange("o p t -> (o p) t"), ots[:, 0, :]).then_inc(g_zdma, 16)
                sp_wait(g_zdma, 16 * (u + 1))
            with sp.Fori(0, NKB) as kb:
                project(kb + NKB, kb)
                with sp.Fori(0, UNITS) as u:
                    row = ot_dram[bass.ds(u, 1), :, :].rearrange("o p t -> (o p) t")
                    sp.dma_start(ots[:, 0, :], row).then_inc(g_old, 16)
                    sp_wait(g_add, 2 * UNITS * kb + 2 * u + 2)
                    sp.dma_start(row, ots[:, 1, :]).then_inc(g_store, 16)
                    sp_wait(g_store, 16 * UNITS * kb + 16 * u + 16)
            with sp.Fori(0, 4) as v:
                rows = ot_dram[bass.ds(2 * v, 2), :, :].rearrange("g (i r) t -> (g i) r t", r=2 * D)
                sp.dma_start(numer[:, :], rows[:, 0:D, :]).then_inc(nd_dma, 16)
                sp.dma_start(denom[:, :], rows[:, D:2 * D, :]).then_inc(nd_dma, 16)
                sp_wait(attn_ready, v + 1)

        def general_pe(pe, scores, scores_T, with_v):
            def project(k, with_values):
                pe.wait_ge(g_x, 32 * k + 32)
                xg = xTs[:, :, 0:NB * KB]
                for c in range(KC):
                    for kc in range(KC):
                        last = nc.tensor.matmul(PS[:, c, :], wqkvs[:, kc, C + P * c:C + P * (c + 1)], xg[:, kc, :],
                                                start=kc == 0, stop=kc == KC - 1)
                if with_values:
                    for b in range(NB):
                        for kt in range(KT):
                            for kc in range(KC):
                                last = nc.tensor.matmul(PS[:, 2 + b, kt * C:(kt + 1) * C],
                                                        xg[:, kc, KB * b + P * kt:KB * b + P * (kt + 1)],
                                                        wqkvs[:, kc, 2 * C:3 * C], start=kc == 0, stop=kc == KC - 1)
                last.then_inc(g_proj, 1)

            pe.wait_ge(q_ready, 4)
            with pe.Fori(0, NKB) as kb:
                project(kb, False)
                with pe.Fori(0, UNITS) as u:
                    n = 2 * QT * UNITS * kb + 2 * QT * u
                    pe.wait_ge(g_kdma, G_KDMA * kb + G_KDMA)
                    for qt in range(QT):
                        for pr in range(2):
                            if qt >= 1:
                                pe.wait_ge(g_red, n + 2 * qt + pr - 1)
                            for i in range(2):
                                last = scores(PS[:, 4 + pr, KB * i:KB * (i + 1)], u, 2 * pr + i, qt)
                            last.then_inc(g_mx, 1)
                    pe.wait_ge(g_red, n + 2 * QT)
            with pe.Fori(0, UNITS) as u:
                pe.wait_ge(g_nm, 5 * u + 5)
                nc.tensor.transpose(PS[0:96, 6, 0:P // 2].bitcast(BF16), nmsp[:, 0, :, :].rearrange("p s m -> p (s m)"),
                                    identb[:, :]).then_inc(g_nmT, 1)
            pe.wait_ge(g_mdma, 16 * UNITS)
            with pe.Fori(0, NKB) as kb:
                project(kb + NKB, True)
                with pe.Fori(0, UNITS) as u:
                    n = CHUNKS * UNITS * kb + CHUNKS * u
                    pe.wait_ge(g_kdma, G_KDMA * (kb + NKB) + G_KDMA)
                    pe.wait_ge(g_vm, kb + 1)
                    pe.wait_ge(g_vu, UNITS * kb + u + 1)
                    for k in range(CHUNKS):
                        scores_T(k % 2, u, k).then_inc(g_st, 1)
                        pe.wait_ge(g_exp, n + k + 1)
                        with_v(k, 0).then_inc(g_pv, 1)
                        if k % 4 == 3:
                            pe.wait_ge(g_add, 2 * UNITS * kb + 2 * u + k // 4 + 1)

        def general_dve(dve, split_maxima, reciprocals):
            def parts_of_k(k):
                dve.wait_ge(g_hi, k + 1)
                nc.vector.tensor_tensor(rest[:, :, :], PS[:, 0:2, :], ksp[:, :, 0, :], ALU.subtract).then_inc(g_rest, 1)
                dve.wait_ge(g_rest, k + 1)
                nc.vector.tensor_copy(ksp[:, :, 1, :], rest[:, :, :]).then_inc(g_mid, 1)
                dve.wait_ge(g_mid, k + 1)
                nc.vector.tensor_tensor(ksp[:, :, 2, :], rest[:, :, :], ksp[:, :, 1, :], ALU.subtract).then_inc(g_lo, 1)

            nc.vector.memset(nmall[:, :, :], 3.0e38).then_inc(g_min, 1)
            with dve.Fori(0, NKB) as kb:
                parts_of_k(kb)
                with dve.Fori(0, UNITS) as u:
                    n = 2 * QT * UNITS * kb + 2 * QT * u
                    dve.wait_ge(g_min, UNITS * kb + u + 1)
                    for qt in range(QT):
                        for pr in range(2):
                            dve.wait_ge(g_mx, n + 2 * qt + pr + 1)
                            nc.vector.tensor_reduce(nmax[:, 0, 2 * pr:2 * pr + 2, qt],
                                                    PS[:, 4 + pr, :].rearrange("p (i t) -> p i t", i=2),
                                                    AX.X, ALU.max, negate=True).then_inc(g_red, 1)
                    dve.wait_ge(g_red, n + 2 * QT)
                    old = nmall[:, bass.ds(u, 1), :].rearrange("p o m -> p (o m)")
                    nc.vector.tensor_tensor(old, old, nmax[:, 0, :, :].rearrange("p i t -> p (i t)"), ALU.min).then_inc(g_min, 1)
            dve.wait_ge(g_min, NKB * UNITS + 1)
            with dve.Fori(0, UNITS) as u:
                split_maxima(nmall[:, bass.ds(u, 1), :].rearrange("p o m -> p (o m)"), 0, g_nm, 5 * u)
                dve.wait_ge(g_nmT, u + 1)
                nc.vector.tensor_copy(nmT[:, 0, :], PS[0:96, 6, 0:P // 2].bitcast(BF16)).then_inc(g_nmTe, 1)
                dve.wait_ge(g_mdma, 16 * u + 16)
            nc.vector.memset(ots[:, 0, :], 0.0).then_inc(g_zero, 1)
            with dve.Fori(0, NKB) as kb:
                parts_of_k(kb + NKB)
                nc.vector.tensor_copy(maskb[:, :, :], maskc[:, :, bass.ds(kb * KT, KT)]).then_inc(g_vcol, 1)
                dve.wait_ge(g_vcol, kb + 1)
                for b in range(NB):
                    for kt in range(KT):
                        nc.vector.tensor_scalar(vaug[:, 4 * b:4 * (b + 1), kt, :, 0:D],
                                                PS[:, 2 + b, C * kt:C * (kt + 1)].rearrange("p (g i d) -> p g i d", i=4, d=D),
                                                maskb[:, b, kt:kt + 1], None, ALU.mult)
                        for g in range(4):
                            last = nc.vector.tensor_copy(vaug[:, 4 * b + g, kt, :, D:2 * D],
                                                         maskb[:, b, kt:kt + 1][:, :, None].to_broadcast([P, 4, D]))
                last.then_inc(g_vm, 1)
                with dve.Fori(0, UNITS) as u:
                    for half in range(2):
                        dve.wait_ge(g_pv, CHUNKS * UNITS * kb + CHUNKS * u + 4 * half + 4)
                        if half == 0:
                            dve.wait_ge(g_old, 16 * UNITS * kb + 16 * u + 16)
                        nc.vector.tensor_tensor(ots[:, 1, BLK * half:BLK * (half + 1)], PS[:, 7, :],
                                                ots[:, 0, BLK * half:BLK * (half + 1)], ALU.add).then_inc(g_add, 1)
            with dve.Fori(0, 4) as v:
                reciprocals(v + 1)

        @block.sync
        def _(sp):
            sp.dma_start(wqkvs[:, :, :], wqkv.rearrange("(k p) n -> p k n", p=P)).then_inc(w_loaded, 16)
            xv = xT.rearrange("(k p) t -> p k t", p=P)
            for i in (0, 1, 3, 2):
                sp.dma_start(xTs[:, :, i * BLK:(i + 1) * BLK], xv[:, :, i * BLK:(i + 1) * BLK]).then_inc(x_loaded[i], 16)
            sp.wait_ge(rows_set, 1)
            sp.wait_ge(consts, 2)
            for b in range(NB):
                sp.dma_start(kst[ONE_ROW:ONE_ROW + 1, H * b:H * (b + 1), :],
                             mbias[0:1, b:b + 1, S - KB:S].to_broadcast([1, H, KB])).then_inc(rows_dma, 16)
            sp.dma_start(qst[ONE_ROW:ONE_ROW + 1, :, :],
                         ones[0:1, None, :].to_broadcast([1, UNITS * 4, S])).then_inc(rows_dma, 16)

            def stack_q(b, c):
                sp.wait_ge(lo_done, SPLITS.index(("q", b, c, 1)) + 1)
                for n, part in enumerate(Q_PARTS):
                    sp.dma_start(qst[D * n:D * (n + 1), H * b + HC * c:H * b + HC * (c + 1), :],
                                 qsp[:, (2 * b + c) % 2, part, :]).then_inc(q_dma[2 * b + c], 16)

            def k_rows(b, c, signal):
                for n, part in enumerate(K_PARTS):
                    sp.dma_start(kst[D * n:D * (n + 1), H * b + HC * c:H * b + HC * (c + 1), :],
                                 ksp[:, c, part, KB * b:KB * (b + 1)]).then_inc(signal, 16)

            def stack_k(b, c):
                sp.wait_ge(lo_done, SPLITS.index(("k", c)) + 1)
                k_rows(b, c, k_dma)

            stack_q(0, 0)
            stack_k(0, 0)
            stack_k(0, 1)
            stack_k(1, 0)
            stack_k(1, 1)
            sp.wait_ge(rows_dma, 16 * (NB + 1))
            sp.wait_ge(k_dma, NB * KC * 16 * len(K_PARTS))
            sp.wait_ge(q_dma[0], N_Q)
            sp.sem_inc(q_ready, 1)
            for v in range(1, 4):
                stack_q(v // 2, v % 2)
                sp.wait_ge(q_dma[v], N_Q)
                sp.sem_inc(q_ready, 1)

            def load_rows(v):
                rows = ot_dram[bass.ds(2 * v, 2), :, :].rearrange("g (i r) t -> (g i) r t", r=2 * D)
                sp.dma_start(numer[:, :], rows[:, 0:D, :]).then_inc(nd_dma, 16)
                sp.dma_start(denom[:, :], rows[:, D:2 * D, :]).then_inc(nd_dma, 16)

            def pair(v, first=False, second=False, last=False):
                for j in range(2):
                    if not (last and j == 1):
                        sp_wait(nmT_evac, 2 * v + j + 2)
                        sp.dma_start(qst[MAX_ROW:ROWS, bass.ds(8 * v + 4 * j + 4, 4), :],
                                     nmT[:, (j + 1) % 2, :]).then_inc(m_dma, 16)
                    if j == 0 and not first:
                        sp_wait(ot_dma[0], 16 * v)
                        sp_wait(ot_dma[1], 16 * v)
                        if not second:
                            sp_wait(attn_ready, v - 1)
                        load_rows(v - 1)
                    sp_wait(ot_evac, 4 * v + 2 * j + 2)
                    sp.dma_start(ot_dram[bass.ds(2 * v + j, 1), :, :].rearrange("o p t -> (o p) t"),
                                 ots[:, j, :]).then_inc(ot_dma[j], 16)

            with nc.sync.register("sp_flag") as r:
                sp.wait_ge(consts, 3)
                sp.reg_load(r, flag[0:1, 0:1])
                with sp.If_eq(r, 0):
                    sp.wait_ge(nmT_evac, 1)
                    sp.dma_start(qst[MAX_ROW:ROWS, 0:4, :], nmT[:, 0, :]).then_inc(m_dma, 16)
                    pair(0, first=True)
                    pair(1, second=True)
                    pair(2)
                    pair(3, last=True)
                    sp.wait_ge(ot_dma[0], 64)
                    sp.wait_ge(ot_dma[1], 64)
                    sp.wait_ge(attn_ready, 3)
                    load_rows(3)
                with sp.If_ne(r, 0):
                    general_sp(sp, xT.rearrange("(k p) (b t) -> p k b t", p=P, b=NB), k_rows)

            xd = x.rearrange("(t p) c -> p t c", p=P)
            od = out.rearrange("(t p) c -> p t c", p=P)
            sp.wait_ge(attn_ready, 4)
            for t in range(2):
                sp.dma_start(xb[t][:, :, :], xd[:, 4 * t:4 * t + 4, :]).then_inc(xb_loaded[t], 16)
            for t in range(4):
                if t < 2:
                    sp.wait_ge(x1_done, t + 1)
                    sp.dma_start(xb[t][:, :, :], xd[:, 4 * t + 8:4 * t + 12, :]).then_inc(xb_loaded[t], 16)
                sp.wait_ge(fin_done, t + 1)
                sp.dma_start(od[:, 4 * t:4 * t + 4, :], fin[t % 2][:, :, :]).then_inc(out_dma[t % 2], 16)
            for s_ in out_dma:
                sp.wait_ge(s_, 32)

        @block.gpsimd
        def _(pool):
            nc.gpsimd.memset(kst[96:ROWS, :, :], 1.0).then_inc(rows_set, 1)
            pool.wait_ge(rows_set, 1)
            pool.wait_ge(consts, 4)
            for u in range(UNITS):
                for kt in range(KT):
                    last = nc.gpsimd.tensor_copy(
                        vaug[:, u, kt, :, D:2 * D],
                        maskc[:, u // 4, QT - KT + kt:QT - KT + kt + 1][:, :, None].to_broadcast([P, 4, D]))
            last.then_inc(vmask_done, 1)
            for n, it in enumerate(SPLITS):
                pool.wait_ge(mid_done, n + 1)
                parts = parts_of(it)
                nc.gpsimd.tensor_tensor(parts[:, 2, :], rest[:, n % 2, :], parts[:, 1, :], ALU.subtract).then_inc(lo_done, 1)

            def normalise(v, n):
                pool.wait_ge(recip_done, n)
                nc.gpsimd.tensor_tensor(attn[:, bass.ds(v, 1), :].rearrange("p o t -> p (o t)"),
                                        numer[:, :], denom[:, :], ALU.mult).then_inc(attn_ready, 1)

            def take_v(u, at, signal):
                src = vaug[:, bass.ds(u, 1), :, :, :].rearrange("p o k i d -> p (o k) (i d)")
                nc.gpsimd.tensor_copy(vunit[:, at, :, :], src).then_inc(signal, 1)

            pool.wait_ge(v_evac, NB * KT)
            pool.wait_ge(vmask_done, 1)
            with nc.gpsimd.register("pool_flag") as r:
                pool.reg_load(r, flag[0:1, 0:1])
                with pool.If_eq(r, 0):
                    take_v(0, 0, vunit_set)
                    take_v(1, 1, vunit_set)
                    with pool.Fori(1, 4) as v:
                        for j in range(2):
                            pool.wait_ge(pv_done, 2 * CHUNKS * v + CHUNKS * (j - 1))
                            take_v(2 * v + j, j, vunit_set)
                        normalise(v - 1, v)
                    normalise(3, 4)
                with pool.If_ne(r, 0):
                    with pool.Fori(0, NKB) as kb:
                        with pool.Fori(0, UNITS) as u:
                            pool.wait_ge(g_vm, kb + 1)
                            take_v(u, 0, g_vu)
                            pool.wait_ge(g_pv, CHUNKS * UNITS * kb + CHUNKS * u + CHUNKS)
                    with pool.Fori(0, 4) as v:
                        normalise(v, v + 1)

            pool.wait_ge(mods_set, 10)

            def finish(t):
                b = t // 2
                pool.wait_ge(z2_done, t + 1)
                if t >= 2:
                    pool.wait_ge(out_dma[t % 2], 16)
                nc.gpsimd.tensor_tensor(fin[t % 2][:, :, :], y2[:, :, :],
                                        mods[:, b, 4:5, :].to_broadcast([P, 4, C]), ALU.mult).then_inc(fin_scaled, 1)
                if t >= 1:
                    pool.wait_ge(fin_done, t)
                nc.gpsimd.tensor_tensor(resid[:, :, :], x1[t % 2][:, :, :],
                                        mods[:, b, 3:4, :].to_broadcast([P, 4, C]), ALU.add).then_inc(resid_set, 1)
                pool.wait_ge(fin_scaled, t + 1)
                pool.wait_ge(resid_set, t + 1)
                nc.gpsimd.tensor_tensor(fin[t % 2][:, :, :], fin[t % 2][:, :, :], resid[:, :, :],
                                        ALU.add).then_inc(fin_done, 1)

            for t in range(4):
                b = t // 2
                pool.wait_ge(xb_loaded[t % 2], 16 * (t // 2 + 1))
                nc.gpsimd.tensor_tensor(xb[t % 2][:, :, :], xb[t % 2][:, :, :],
                                        mods[:, b, 0:1, :].to_broadcast([P, 4, C]), ALU.add).then_inc(xb_set, 1)
                pool.wait_ge(z1_done, t + 1)
                if t >= 2:
                    pool.wait_ge(fin_done, t - 1)
                nc.gpsimd.tensor_tensor(x1[t % 2][:, :, :], y1[:, :, :],
                                        mods[:, b, 1:2, :].to_broadcast([P, 4, C]), ALU.mult).then_inc(x1_scaled, 1)
                pool.wait_ge(xb_set, t + 1)
                pool.wait_ge(x1_scaled, t + 1)
                nc.gpsimd.tensor_tensor(x1[t % 2][:, :, :], x1[t % 2][:, :, :], xb[t % 2][:, :, :],
                                        ALU.add).then_inc(x1_done, 1)
                if t >= 1:
                    finish(t - 1)
            finish(3)

        @block.tensor
        def _(pe):
            pe.wait_ge(w_loaded, 16)
            keys = xTs[:, :, :].rearrange("p k (b t) -> p k b t", b=NB)[:, :, :, S - KB:S]
            for n, it in enumerate(ITEMS):
                if n >= 8:
                    pe.wait_ge(rest_done, SPLITS.index(ITEMS[n - 8]) + 1)
                bank = PS[:, n % 8, :]
                for k in range(KC):
                    if it[0] == "q":
                        _, b, c, half = it
                        pe.wait_ge(x_loaded[2 * b + half], 16)
                        last = nc.tensor.matmul(bank, wqkvs[:, k, P * c:P * (c + 1)],
                                                xTs[:, k, b * S + half * BLK:b * S + (half + 1) * BLK],
                                                start=k == 0, stop=k == KC - 1)
                    elif it[0] == "k":
                        c = it[1]
                        pe.wait_ge(x_loaded[1], 16)
                        pe.wait_ge(x_loaded[3], 16)
                        last = nc.tensor.matmul(bank.rearrange("p (b t) -> p b t", b=NB),
                                                wqkvs[:, k, C + P * c:C + P * (c + 1)],
                                                keys[:, k, :, :], start=k == 0, stop=k == KC - 1)
                if it[0] == "v":
                    b = it[1]
                    for kt in range(KT):
                        for k in range(KC):
                            last = nc.tensor.matmul(bank[:, kt * C:(kt + 1) * C], keys[:, k, b, P * kt:P * (kt + 1)],
                                                    wqkvs[:, k, 2 * C:3 * C], start=k == 0, stop=k == KC - 1)
                last.then_inc(v_done if it[0] == "v" else proj_done, 1)

            pe.wait_ge(ada_loaded, 16 * 5)
            pe.wait_ge(rest_done, len(SPLITS))
            pe.wait_ge(v_evac, NB * KT)
            for m in range(KC):
                for k in range(KC):
                    last = nc.tensor.matmul(PS[:, 0, NB * m:NB * (m + 1)], wa1s[:, k, P * m:P * (m + 1)],
                                            cTs[:, k, :], start=k == 0, stop=k == KC - 1)
            last.then_inc(ada1_done, 1)
            pe.wait_ge(dve_step, 4)
            for n in range(6):
                b, part = n // 3, n % 3
                for k in range(KC):
                    last = nc.tensor.matmul(PS[:, 1 + n, :], sil[:, 2, NB * k + b:NB * k + b + 1].to_broadcast([P, P]),
                                            wa2s[:, k, BLK * part:BLK * (part + 1)], start=k == 0, stop=k == KC - 1)
                last.then_inc(ada2_done, 1)

            def scores(bank, u, i, tile):
                return nc.tensor.matmul(bank, qst[0:MAX_ROW, bass.ds(4 * u + i, 1), P * tile:P * (tile + 1)].rearrange("p o t -> p (o t)"),
                                        kst[0:MAX_ROW, bass.ds(4 * u + i, 1), :].rearrange("p o t -> p (o t)"),
                                        start=True, stop=True)

            def scores_T(slot_, u, k):
                half, pr, kt = chunk_of(k)
                for i in range(2):
                    h = 4 * u + 2 * pr + i
                    last = nc.tensor.matmul(PS[:, 2 * slot_ + i, :],
                                            kst[0:ROWS, bass.ds(h, 1), P * kt:P * (kt + 1)].rearrange("p o t -> p (o t)"),
                                            qst[0:ROWS, bass.ds(h, 1), BLK * half:BLK * (half + 1)].rearrange("p o t -> p (o t)"),
                                            start=True, stop=True)
                return last

            def with_v(k, at):
                half, pr, kt = chunk_of(k)
                for i in range(2):
                    h = 2 * pr + i
                    last = nc.tensor.matmul(PS[32 * h:32 * (h + 1), 7, :], vunit[:, at, kt, 32 * h:32 * (h + 1)],
                                            probs[:, k % 4, i, :], start=kt == 0, stop=kt == KT - 1, tile_position=(0, 32 * h))
                return last

            def maxima(u, qt):
                for pr in range(2):
                    pe.wait_ge(red_done, slot(u, qt, pr) - 1)
                    for i in range(2):
                        last = scores(PS[:, 4 + pr, KB * i:KB * (i + 1)], u, 2 * pr + i, qt)
                    last.then_inc(mx_done, 1)

            def transpose_maxima(u, at):
                pe.wait_ge(nm_split, 5 * u + 5)
                nc.tensor.transpose(PS[0:96, 6, 0:P // 2].bitcast(BF16), nmsp[:, at, :, :].rearrange("p s m -> p (s m)"),
                                    identb[:, :]).then_inc(nmT_done, 1)

            def unit(v, j, first=False, last=False):
                u = 2 * v + j
                for k in range(CHUNKS):
                    if k == 0:
                        pe.wait_ge(m_dma, 16 * u + 16)
                    if not (first and k < 2):
                        pe.wait_ge(exp_done, CHUNKS * u + k - 1)
                    scores_T(k % 2, u, k).then_inc(st_done, 1)
                    if k < 4 and not (last and j == 1):
                        maxima(u + 1, k + 4)
                    if k >= 4 and not last:
                        if k == 4 and j == 0:
                            pe.wait_ge(q_ready, v + 2)
                        maxima(u + 2, k - 4)
                    if k == 0 and not first:
                        products(u - 1, (j + 1) % 2, CHUNKS - 1)
                    if k > 0:
                        products(u, j, k - 1)
                    if k == 4 and not (last and j == 1):
                        transpose_maxima(u + 1, (j + 1) % 2)

            def products(u, at, k):
                pe.wait_ge(exp_done, CHUNKS * u + k + 1)
                if k == 0:
                    pe.wait_ge(vunit_set, u + 1)
                if k % 4 == 0:
                    pe.wait_ge(ot_evac, 2 * u + k // 4)
                with_v(k, at).then_inc(pv_done, 1)

            with nc.tensor.register("pe_flag") as r:
                pe.wait_ge(consts, 5)
                pe.reg_load(r, flag[0:1, 0:1])
                pe.wait_ge(mods_set, 6)
                pe.wait_ge(q_ready, 1)
                with pe.If_eq(r, 0):
                    for qt in range(QT):
                        for pr in range(2):
                            if slot(0, qt, pr) >= 2:
                                pe.wait_ge(red_done, slot(0, qt, pr) - 1)
                            for i in range(2):
                                last = scores(PS[:, 4 + pr, KB * i:KB * (i + 1)], 0, 2 * pr + i, qt)
                            last.then_inc(mx_done, 1)
                    for qt in range(4):
                        maxima(1, qt)
                    transpose_maxima(0, 0)
                    unit(0, 0, first=True)
                    unit(0, 1)
                    with pe.Fori(1, 3) as v:
                        unit(v, 0)
                        unit(v, 1)
                    unit(3, 0, last=True)
                    unit(3, 1, last=True)
                    products(7, 1, CHUNKS - 1)
                with pe.If_ne(r, 0):
                    general_pe(pe, scores, scores_T, with_v)

            pe.wait_ge(mlp_loaded, 16 * 6)

            def project_out(t):
                pe.wait_ge(attn_ready, 2 * (t // 2) + 2)
                for tile in range(4):
                    if tile % 2 == 0 and t >= 1:
                        pe.wait_ge(y1_set, 2 * t - 1 + tile // 2)
                    at = BLK * (t % 2) + P * tile
                    for c in range(KC):
                        last = nc.tensor.matmul(PS[:, tile // 2, C * (tile % 2):C * (tile % 2 + 1)],
                                                attn[:, 2 * (t // 2) + c, at:at + P], wps[:, c, :],
                                                start=c == 0, stop=c == KC - 1)
                    if tile % 2:
                        last.then_inc(y1_mm, 1)

            def transpose_x1(t):
                pe.wait_ge(x1_done, t + 1)
                if t >= 1:
                    pe.wait_ge(x1T_set, 2 * t)
                for c in range(KC):
                    for tile in range(4):
                        last = nc.tensor.transpose(PS[:, 2 + c, P * tile:P * (tile + 1)],
                                                   x1[t % 2][:, tile, P * c:P * (c + 1)], identf[:, :])
                    last.then_inc(x1T_mm, 1)

            def fc1(t):
                pe.wait_ge(x1T_set, 2 * t + 2)
                for f in range(FF // P):
                    n = FF // P * t + f
                    if n >= 2:
                        pe.wait_ge(gelu_done, n - 1)
                    for c in range(KC):
                        last = nc.tensor.matmul(PS[:, 4 + f % 2, :], w1s[:, c, P * f:P * (f + 1)], x1T[t % 2][:, c, :],
                                                start=c == 0, stop=c == KC - 1)
                    last.then_inc(fc1_mm, 1)

            def fc2(t):
                for tile in range(4):
                    if tile % 2 == 0 and t >= 1:
                        pe.wait_ge(y2_set, 2 * t - 1 + tile // 2)
                    for f in range(FF // P):
                        pe.wait_ge(gelu_done, FF // P * t + f + 1)
                        last = nc.tensor.matmul(PS[:, 6 + tile // 2, C * (tile % 2):C * (tile % 2 + 1)],
                                                hid[t % 2][:, f, P * tile:P * (tile + 1)], w2s[:, f, :],
                                                start=f == 0, stop=f == FF // P - 1)
                    if tile % 2:
                        last.then_inc(fc2_mm, 1)

            project_out(0)
            transpose_x1(0)
            for t in range(4):
                if t < 3:
                    project_out(t + 1)
                fc1(t)
                if t < 3:
                    transpose_x1(t + 1)
                fc2(t)

        @block.scalar
        def _(act):
            act.dma_start(mrow8[0:1, :, :], mask.rearrange("(o b) s -> o b s", o=1)).then_inc(mask_loaded, 16)
            act.dma_start(mask8[:, :], mask_cols).then_inc(mask_loaded, 16)
            act.dma_start(identf[:, :], ident).then_inc(mask_loaded, 16)
            act.dma_start(cTs[:, :, :], cT.rearrange("(k p) b -> p k b", p=P)).then_inc(ada_loaded, 16)
            act.dma_start(wa1s[:, :, :], wa1.rearrange("(k p) n -> p k n", p=P)).then_inc(ada_loaded, 16)
            act.dma_start(ba1s[:, :], ba1).then_inc(ada_loaded, 16)
            act.dma_start(wa2s[:, :, :], wa2.rearrange("(k p) n -> p k n", p=P)).then_inc(ada_loaded, 16)
            act.dma_start(ba2s[:, :], ba2[None, :].to_broadcast([P, 6 * C])).then_inc(ada_loaded, 16)

            for it in ITEMS:
                if it[0] == "v":
                    b = it[1]
                    act.wait_ge(v_done, b + 1)
                    act.wait_ge(consts, 4)
                    for kt in range(KT):
                        nc.scalar.activation(vaug[:, 4 * b:4 * (b + 1), kt, :, 0:D],
                                             PS[:, bank_of[it], C * kt:C * (kt + 1)].rearrange("p (g i d) -> p g i d", i=4, d=D),
                                             ACT.Copy, scale=maskc[:, b, QT - KT + kt:QT - KT + kt + 1]).then_inc(v_evac, 1)
                    continue
                act.wait_ge(proj_done, SPLITS.index(it) + 1)
                if it[0] == "q" and it[1] == 1:
                    act.wait_ge(q_dma[it[2]], N_Q)
                nc.scalar.copy(parts_of(it)[:, 0, :], PS[:, bank_of[it], :]).then_inc(hi_done, 1)

            act.wait_ge(dve_step, 1)
            nc.scalar.activation(sil[:, 1, :], sil[:, 0, :], ACT.Exp, scale=-1.0).then_inc(sil_exp, 1)
            act.dma_start(wps[:, :, :], wp.rearrange("(k p) n -> p k n", p=P)).then_inc(mlp_loaded, 16)
            act.dma_start(bps[:, :], bp[None, :].to_broadcast([P, C])).then_inc(mlp_loaded, 16)
            act.dma_start(w1s[:, :, :], w1.rearrange("(k p) n -> p k n", p=P)).then_inc(mlp_loaded, 16)
            act.dma_start(b1s[:, :], b1).then_inc(mlp_loaded, 16)
            act.dma_start(w2s[:, :, :], w2.rearrange("(k p) n -> p k n", p=P)).then_inc(mlp_loaded, 16)
            act.dma_start(b2s[:, :], b2[None, :].to_broadcast([P, C])).then_inc(mlp_loaded, 16)

            def exps(slot_, k, signal):
                nc.scalar.activation(probs[:, k % 4, :, :], PS[:, 2 * slot_:2 * slot_ + 2, :], ACT.Exp,
                                     scale=float(D) ** -0.5).then_inc(signal, 1)

            def rows_out(v, j, half, first):
                q = 4 * v + 2 * j + half
                act.wait_ge(pv_done, 4 * q + 4)
                if half == 0 and not first:
                    act.wait_ge(ot_dma[j], 16 * v)
                nc.scalar.copy(ots[:, j, BLK * half:BLK * (half + 1)], PS[:, 7, :]).then_inc(ot_evac, 1)

            def unit(v, j, first=False):
                u = 2 * v + j
                for k in range(CHUNKS):
                    act.wait_ge(st_done, CHUNKS * u + k + 1)
                    if not (first and j == 0 and k < 4):
                        act.wait_ge(pv_done, CHUNKS * u + k - 3)
                    exps(k % 2, k, exp_done)
                    if k == 0 and not (first and j == 0):
                        rows_out(v if j else v - 1, 1 - j, 1, first)
                    if k == 4:
                        rows_out(v, j, 0, first)

            with nc.scalar.register("act_flag") as r:
                act.wait_ge(consts, 3)
                act.reg_load(r, flag[0:1, 0:1])
                with act.If_eq(r, 0):
                    unit(0, 0, first=True)
                    unit(0, 1, first=True)
                    with act.Fori(1, 4) as v:
                        unit(v, 0)
                        unit(v, 1)
                    rows_out(3, 1, 1, False)
                with act.If_ne(r, 0):
                    def high_parts(k):
                        act.wait_ge(g_proj, k + 1)
                        nc.scalar.copy(ksp[:, :, 0, :], PS[:, 0:2, :]).then_inc(g_hi, 1)

                    with act.Fori(0, NKB) as kb:
                        high_parts(kb)
                    with act.Fori(0, NKB) as kb:
                        high_parts(kb + NKB)
                        with act.Fori(0, UNITS) as u:
                            n = CHUNKS * UNITS * kb + CHUNKS * u
                            for k in range(CHUNKS):
                                act.wait_ge(g_st, n + k + 1)
                                exps(k % 2, k, g_exp)
                                act.wait_ge(g_pv, n + k + 1)

            act.wait_ge(mlp_loaded, 16 * 6)

            def x1T_out(t):
                for c in range(KC):
                    act.wait_ge(x1T_mm, 2 * t + c + 1)
                    nc.scalar.copy(x1T[t % 2][:, c, :], PS[:, 2 + c, :]).then_inc(x1T_set, 1)

            x1T_out(0)
            for t in range(4):
                for f in range(FF // P):
                    act.wait_ge(fc1_mm, FF // P * t + f + 1)
                    if t >= 2 and f == 0:
                        act.wait_ge(fc2_mm, 2 * t - 2)
                    nc.scalar.activation(hid[t % 2][:, f, :], PS[:, 4 + f % 2, :], ACT.Gelu,
                                         bias=b1s[:, f:f + 1]).then_inc(gelu_done, 1)
                if t < 3:
                    x1T_out(t + 1)

        @block.vector
        def _(dve):
            steps = [0]

            def step(ins):
                steps[0] += 1
                ins.then_inc(dve_step, 1)
                dve.wait_ge(dve_step, steps[0])

            dve.wait_ge(mask_loaded, 48)
            nc.vector.tensor_scalar(mbias[0:1, :, :], mrow8[0:1, :, :], MASKED, -MASKED, ALU.mult, ALU.add).then_inc(consts, 1)
            nc.vector.memset(ones[0:1, :], 1.0).then_inc(consts, 1)
            nc.vector.tensor_reduce(flagf[0:1, :], mrow8[0:1, :, 0:S - KEYS_FAST], AX.XY, ALU.max).then_inc(flag_step, 1)
            dve.wait_ge(flag_step, 1)
            nc.vector.tensor_copy(flag[0:1, :], flagf[0:1, :]).then_inc(consts, 1)
            nc.vector.tensor_copy(maskc[:, :, :], mask8[:, :].rearrange("p (b t) -> p b t", b=NB)).then_inc(consts, 1)
            nc.vector.tensor_copy(identb[:, :], identf[:, :]).then_inc(consts, 1)

            for n, it in enumerate(SPLITS):
                parts = parts_of(it)
                dve.wait_ge(hi_done, n + 1)
                if n >= 2:
                    dve.wait_ge(lo_done, n - 1)
                nc.vector.tensor_tensor(rest[:, n % 2, :], PS[:, bank_of[it], :], parts[:, 0, :],
                                        ALU.subtract).then_inc(rest_done, 1)
                dve.wait_ge(rest_done, n + 1)
                nc.vector.tensor_copy(parts[:, 1, :], rest[:, n % 2, :]).then_inc(mid_done, 1)

            dve.wait_ge(ada_loaded, 80)
            dve.wait_ge(ada1_done, 1)
            step(nc.vector.tensor_tensor(sil[:, 0, :].rearrange("p (k b) -> p k b", b=NB),
                                         PS[:, 0, 0:KC * NB].rearrange("p (k b) -> p k b", b=NB),
                                         ba1s[:, :, None].to_broadcast([P, KC, NB]), ALU.add))
            dve.wait_ge(sil_exp, 1)
            step(nc.vector.tensor_scalar_add(sil[:, 1, :], sil[:, 1, :], 1.0))
            step(nc.vector.reciprocal(sil[:, 1, :], sil[:, 1, :]))
            step(nc.vector.tensor_tensor(sil[:, 2, :], sil[:, 0, :], sil[:, 1, :], ALU.mult))
            for n in range(6):
                b, part = n // 3, n % 3
                dve.wait_ge(ada2_done, n + 1)
                nc.vector.tensor_tensor(mods[:, b, 2 * part:2 * part + 2, :].rearrange("p m c -> p (m c)"),
                                        PS[:, 1 + n, :], ba2s[:, BLK * part:BLK * (part + 1)], ALU.add).then_inc(mods_set, 1)
            dve.wait_ge(mods_set, 6)
            for h0 in (0, 3):
                gate = mods[:, :, h0 + 2, :]
                nc.vector.tensor_tensor(mods[:, :, h0, :], mods[:, :, h0, :], gate, ALU.mult).then_inc(mods_set, 1)
                nc.vector.scalar_tensor_tensor(mods[:, :, h0 + 1, :], mods[:, :, h0 + 1, :], 1.0, gate,
                                               ALU.add, ALU.mult).then_inc(mods_set, 1)

            def split_maxima(src, at, signal, base):
                rs = nmrest[:, at, :]
                nc.vector.tensor_copy(nmsp[:, at, 0, :], src).then_inc(signal, 1)
                dve.wait_ge(signal, base + 1)
                nc.vector.tensor_tensor(rs, src, nmsp[:, at, 0, :], ALU.subtract).then_inc(signal, 1)
                dve.wait_ge(signal, base + 2)
                nc.vector.tensor_copy(nmsp[:, at, 1, :], rs).then_inc(signal, 1)
                dve.wait_ge(signal, base + 3)
                nc.vector.tensor_tensor(rs, rs, nmsp[:, at, 1, :], ALU.subtract).then_inc(signal, 1)
                dve.wait_ge(signal, base + 4)
                nc.vector.tensor_copy(nmsp[:, at, 2, :], rs).then_inc(signal, 1)

            def maxima(u, at, qt):
                for pr in range(2):
                    dve.wait_ge(mx_done, slot(u, qt, pr) + 1)
                    nc.vector.tensor_reduce(nmax[:, at, 2 * pr:2 * pr + 2, qt],
                                            PS[:, 4 + pr, :].rearrange("p (i t) -> p i t", i=2),
                                            AX.X, ALU.max, negate=True).then_inc(red_done, 1)

            def split(u, at):
                dve.wait_ge(red_done, slot(u, QT - 1, 1) + 1)
                split_maxima(nmax[:, at, :, :].rearrange("p i t -> p (i t)"), at, nm_split, 5 * u)

            def transposed(u, at, first=False):
                dve.wait_ge(nmT_done, u + 1)
                if not first:
                    dve.wait_ge(m_dma, 16 * u - 16)
                nc.vector.tensor_copy(nmT[:, at, :], PS[0:96, 6, 0:P // 2].bitcast(BF16)).then_inc(nmT_evac, 1)

            def unit(v, j, first=False, last=False):
                u = 2 * v + j
                for k in range(CHUNKS):
                    if k < 4 and not (last and j == 1):
                        maxima(u + 1, 1 - j, k + 4)
                    if k == 3 and not (last and j == 1):
                        split(u + 1, 1 - j)
                    if k >= 4 and not last:
                        maxima(u + 2, j, k - 4)
                    if k == 4 and not (last and j == 1):
                        transposed(u + 1, 1 - j, first and j == 0)
                    if k == 5 and j == 1 and not first:
                        reciprocals(v)

            def reciprocals(n):
                dve.wait_ge(nd_dma, 32 * n)
                nc.vector.reciprocal(denom[:, :], denom[:, :]).then_inc(recip_done, 1)

            with nc.vector.register("dve_flag") as r:
                dve.wait_ge(consts, 3)
                dve.reg_load(r, flag[0:1, 0:1])
                with dve.If_eq(r, 0):
                    for qt in range(QT):
                        maxima(0, 0, qt)
                    split(0, 0)
                    for qt in range(4):
                        maxima(1, 1, qt)
                    transposed(0, 0, first=True)
                    unit(0, 0, first=True)
                    unit(0, 1, first=True)
                    with dve.Fori(1, 3) as v:
                        unit(v, 0)
                        unit(v, 1)
                    unit(3, 0, last=True)
                    unit(3, 1, last=True)
                    reciprocals(4)
                with dve.If_ne(r, 0):
                    general_dve(dve, split_maxima, reciprocals)

            def norm(t, half, banks, y, bias, mm, y_set, z_done, used):
                if t >= 1:
                    dve.wait_ge(used, t)
                for i in range(2):
                    dve.wait_ge(mm, 2 * t + i + 1)
                    nc.vector.tensor_tensor(y[:, 2 * i:2 * i + 2, :],
                                            PS[:, banks + i, :].rearrange("p (t c) -> p t c", t=2),
                                            bias[:, None, :].to_broadcast([P, 2, C]), ALU.add).then_inc(y_set, 1)
                dve.wait_ge(y_set, 2 * t + 2)
                for i in range(4):
                    ins = nc.vector.bn_stats(stats[:, i, :], y[:, i, :])
                step(ins)
                for i in range(4):
                    ins = nc.vector.bn_aggr(mv[:, half, i, :], stats[:, i, :])
                step(ins)
                var, g, w, a = mv[:, half, :, 1], nwt[:, 0, :], nwt[:, 1, :], nwt[:, 2, :]
                step(nc.vector.tensor_scalar_add(a, var, EPS))
                step(nc.vector.tensor_scalar(w, a, -0.5, None, ALU.mult))
                step(nc.vector.tensor_single_scalar(nwt[:, 3, :].bitcast(I32), a.bitcast(I32), 1, ALU.logical_shift_right))
                step(nc.vector.tensor_scalar(g.bitcast(I32), nwt[:, 3, :].bitcast(I32), -1.0, float(0x5F3759DF), ALU.mult, ALU.add))
                for _ in range(3):
                    step(nc.vector.tensor_tensor(a, g, g, ALU.mult))
                    step(nc.vector.tensor_tensor(a, a, w, ALU.mult))
                    step(nc.vector.scalar_tensor_tensor(g, a, 1.5, g, ALU.add, ALU.mult))
                for i in range(4):
                    ins = nc.vector.tensor_scalar(y[:, i, :], y[:, i, :], mv[:, half, i, 0:1], nwt[:, 0, i:i + 1],
                                                  ALU.subtract, ALU.mult)
                ins.then_inc(z_done, 1)

            dve.wait_ge(mlp_loaded, 16 * 6)

            def norm1(t):
                norm(t, 0, 0, y1, bps, y1_mm, y1_set, z1_done, x1_scaled)

            def norm2(t):
                norm(t, 1, 6, y2, b2s, fc2_mm, y2_set, z2_done, fin_scaled)

            norm1(0)
            norm1(1)
            for t in range(4):
                norm2(t)
                if t < 2:
                    norm1(t + 2)

INPUTS = ("xT", "x", "cT", "mask", "mask_cols", "ident", "wqkv", "wp", "bp", "w1", "b1", "w2", "b2", "wa1", "ba1", "wa2", "ba2")


def kernel(x, cond_1024, mask_BxS_bk0, L0_cond_qkv_w, L0_cond_proj_w, L0_cond_proj_b, L0_cond_fc1_w, L0_cond_fc1_b,
           L0_cond_fc2_w, L0_cond_fc2_b, L0_cond_ada1_w, L0_cond_ada1_b, L0_cond_ada2_w, L0_cond_ada2_b):
    import concourse.bacc as bacc
    from concourse.bass_utils import run_bass_kernel_spmd

    tokens = np.asarray(x).reshape(T, C)
    mask = np.asarray(mask_BxS_bk0)
    qkv = np.asarray(L0_cond_qkv_w)
    qk = qkv[:, :2 * C].reshape(C, 2, KC, HC, D).transpose(0, 1, 2, 4, 3).reshape(C, 2 * C)
    arrays = {
        "xT": tokens.T, "x": tokens, "cT": np.asarray(cond_1024).T, "mask": mask,
        "mask_cols": mask.reshape(NB * QT, P).T, "ident": np.eye(P, dtype=np.float32),
        "wqkv": np.concatenate([qk, qkv[:, 2 * C:]], axis=1), "wp": L0_cond_proj_w, "bp": L0_cond_proj_b,
        "w1": L0_cond_fc1_w, "b1": np.asarray(L0_cond_fc1_b).reshape(FF // P, P).T, "w2": L0_cond_fc2_w, "b2": L0_cond_fc2_b,
        "wa1": L0_cond_ada1_w, "ba1": np.asarray(L0_cond_ada1_b).reshape(KC, P).T, "wa2": L0_cond_ada2_w, "ba2": L0_cond_ada2_b,
    }
    arrays = {n: np.ascontiguousarray(a) for n, a in arrays.items()}
    nc = bacc.Bacc("TRN2", target_bir_lowering=False, num_devices=1)
    aps = [nc.dram_tensor(f"in_{n}", arrays[n].shape, mybir.dt.from_np(arrays[n].dtype), kind="ExternalInput").ap()
           for n in INPUTS]
    result = nc.dram_tensor("result", (T, C), F32, kind="ExternalOutput").ap()
    cond_block(nc, *aps, result)
    r = run_bass_kernel_spmd(nc, [{f"in_{n}": a for n, a in arrays.items()}], core_ids=[0])
    return r.results[0]["result"].reshape(NB, S, C)
```

```python
from contextlib import ExitStack

import numpy as np

import concourse.bass as bass
from concourse import mybir

F32 = mybir.dt.float32
BF16 = mybir.dt.bfloat16
I32 = mybir.dt.int32
U8 = mybir.dt.uint8
ALU = mybir.AluOpType
ACT = mybir.ActivationFunctionType
AX = mybir.AxisListType

NB, S, C, H = 2, 1024, 256, 16
D = C // H
FF = 4 * C
EPS = 1e-5
P = 128
KC = C // P
HC = P // D
T = NB * S
BLK = 512
KB = 256
NKB = S // KB
KEYS_FAST = KB
KT = KB // P
UNITS = NB * H // 4
QT = S // P
CHUNKS = 8
ROWS = 100
ONE_ROW, MAX_ROW = 96, 97
LEAD_USES = 28
SPLIT_LAG = 5
LAST_STEPS = 11
MASKED = 1.0e30
Q_PARTS = (0, 1, 2, 0, 1, 0)
K_PARTS = (0, 0, 0, 1, 1, 2)


def cond_block(nc, xT, x, cT, mask, mask_cols, ident, wqkv, wp, bp, w1, b1, w2, b2, wa1, ba1, wa2, ba2, out):
    recip_dram = nc.dram_tensor("reciprocals", (4, HC, S), F32, kind="Internal").ap()
    ot_dram = nc.dram_tensor("attention_rows", (UNITS, P, S), F32, kind="Internal").ap()
    with ExitStack() as ctx:
        def sb(name, shape, dt):
            return ctx.enter_context(nc.sbuf_tensor(name, shape, dt))

        def sem(name):
            return ctx.enter_context(nc.semaphore(name))

        def view(region, at, shape, dt=F32):
            size = int(np.prod(shape)) * (1 if dt == F32 else 0.5)
            v = region[:, at:at + int(size)]
            if dt != F32:
                v = v.bitcast(dt)
            names = "abcd"[:len(shape)]
            if len(shape) > 1:
                v = v.rearrange(f"p ({' '.join(names)}) -> p {' '.join(names)}",
                                **{n: s for n, s in zip(names, shape)})
            return v

        r_qst = sb("r_qst", [P, UNITS * 4 * S // 2], F32)
        qst = view(r_qst, 0, [UNITS * 4, S], BF16)
        kst = sb("kst", [P, H, NB, KB], BF16)
        vaug = sb("vaug", [P, UNITS, KT, 4, 2 * D], F32)
        vunit = sb("vunit", [P, KT, 4 * 2 * D], F32)
        r_x = sb("r_x", [P, KC * T], F32)
        xTs = view(r_x, 0, [KC, T])
        probs = view(r_x, 0, [4, 2, BLK])
        r_split = sb("r_split", [P, 7168], F32)
        qsp = view(r_split, 0, [3, 3, S], BF16)
        ksp = view(r_split, 4608, [KC, 3, NB * KB], BF16)
        rest = view(r_split, 6144, [2, BLK])
        numer = view(r_split, 0, [S])
        recips = view(r_split, 1024, [S])
        denom = view(r_split, 2048, [HC * S // P])
        r_ots = sb("r_ots", [P, 2 * S], F32)
        ots = view(r_ots, 0, [2, S])
        wa1s = view(r_ots, 0, [KC, C])
        mrow8 = r_ots[0:1, 1024:1536].bitcast(U8).rearrange("p (b s) -> p b s", b=NB)
        ones = r_ots[0:1, 1536:2048].bitcast(BF16)
        r_attn = sb("r_attn", [P, 4608], F32)
        attn = view(r_attn, 0, [4, S])
        wa2s = view(r_attn, 0, [KC, 6 * C])
        ba2s = view(r_attn, 3072, [6 * C])
        wqkvs = sb("wqkvs", [P, KC, 3 * C], F32)
        wps = sb("wps", [P, KC, C], F32)
        w1s = sb("w1s", [P, KC, FF], F32)
        w2s = sb("w2s", [P, FF // P, C], F32)
        cTs = sb("cTs", [P, KC, NB], F32)
        b1s = sb("b1s", [P, FF // P], F32)
        ba1s = sb("ba1s", [P, KC], F32)
        bps = sb("bps", [P, C], F32)
        b2s = sb("b2s", [P, C], F32)
        mods = sb("mods", [P, NB, 6, C], F32)
        sil = sb("sil", [P, 3, KC * NB], F32)
        identf = sb("identf", [P, P], F32)
        identb = sb("identb", [P, P], BF16)
        mask8 = sb("mask8", [P, NB * QT], U8)
        maskc = sb("maskc", [P, NB, QT], F32)
        maskb = sb("maskb", [P, NB, KT], F32)
        mbias = sb("mbias", [1, NB, S], BF16)
        flagf = sb("flagf", [1, 1], F32)
        flag = sb("flag", [1, 1], I32)
        nmax = sb("nmax", [P, 2, 4, QT], F32)
        nmsp = sb("nmsp", [P, 2, 3, 4 * QT], BF16)
        nmrest = sb("nmrest", [P, 2, 4 * QT], F32)
        nmT = sb("nmT", [96, 2, P], BF16)
        nmall = sb("nmall", [P, UNITS, 4 * QT], F32)
        PS = ctx.enter_context(nc.psum_tensor("PS", [P, 8, BLK], F32))

        hid = [view(r_qst, 12288 * i, [FF // P, BLK]) for i in range(2)]
        xb = [view(r_qst, 4096 + 1024 * i, [4, C]) for i in range(2)]
        y1 = view(r_qst, 6144, [4, C])
        y2 = view(r_qst, 7168, [4, C])
        x1 = [view(r_qst, 8192 + 1024 * i, [4, C]) for i in range(2)]
        x1T = [view(r_qst, 10240 + 1024 * i, [KC, BLK]) for i in range(2)]
        fin = [view(r_x, 1024 * i, [4, C]) for i in range(2)]
        resid = [view(r_split, 4608 + 1024 * i, [4, C]) for i in range(2)]
        stats = sb("stats", [P, 4, 6], F32)
        mv = sb("mv", [P, 2, 4, 2], F32)
        nwt = sb("nwt", [P, 4, 4], F32)

        w_loaded, x_loaded = sem("w_loaded"), [sem(f"x_loaded{i}") for i in range(4)]
        mask_loaded, mlp_loaded = sem("mask_loaded"), sem("mlp_loaded")
        ada_loaded, ada2_loaded, ba2_loaded = sem("ada_loaded"), sem("ada2_loaded"), sem("ba2_loaded")
        consts = sem("consts")
        rows_dma = sem("rows_dma")
        proj_done, v_done = sem("proj_done"), sem("v_done")
        hi_done = sem("hi_done")
        rest_done, mid_done = sem("rest_done"), sem("mid_done")
        lo_done = sem("lo_done")
        v_evac = sem("v_evac")
        vmask_done = sem("vmask_done")
        q_dma, k_dma = [sem(f"q_dma{i}") for i in range(4)], [sem(f"k_dma{i}") for i in range(2)]
        ada1_done, ada2_done = sem("ada1_done"), sem("ada2_done")
        sil_exp = sem("sil_exp")
        mods_raw, mods_set = sem("mods_raw"), sem("mods_set")
        mx_done, red_done = sem("mx_done"), sem("red_done")
        nm_split, m_dma = sem("nm_split"), sem("m_dma")
        st_done, exp_done = sem("st_done"), sem("exp_done")
        pv_done, ot_evac = sem("pv_done"), sem("ot_evac")
        ot_dma, nd_dma = [sem("ot_dma0"), sem("ot_dma1")], sem("nd_dma")
        den_dma, recip_done, recip_dma = sem("den_dma"), sem("recip_done"), sem("recip_dma")
        attn_ready = sem("attn_ready")
        flag_step = sem("flag_step")
        sp_passed = sem("sp_passed")
        dve_step = sem("dve_step")
        g_x, g_proj, g_hi, g_mid, g_lo, g_kdma = (sem(n) for n in ("g_x", "g_proj", "g_hi", "g_mid", "g_lo", "g_kdma"))
        g_mx, g_red, g_min = (sem(n) for n in ("g_mx", "g_red", "g_min"))
        g_nm, g_nmT, g_nmTe, g_mdma = (sem(n) for n in ("g_nm", "g_nmT", "g_nmTe", "g_mdma"))
        g_rest, g_vm, g_vcol, g_vu, g_zero, g_zdma, g_old = (sem(n) for n in (
            "g_rest", "g_vm", "g_vcol", "g_vu", "g_zero", "g_zdma", "g_old"))
        g_st, g_exp, g_pv, g_add, g_store = (sem(n) for n in ("g_st", "g_exp", "g_pv", "g_add", "g_store"))
        xb_loaded, out_dma = [sem("xb_loaded0"), sem("xb_loaded1")], [sem("out_dma0"), sem("out_dma1")]
        y1_mm, x1T_mm, fc1_mm, fc2_mm = (sem(n) for n in ("y1_mm", "x1T_mm", "fc1_mm", "fc2_mm"))
        y1_set, z1_done, y2_set, z2_done = (sem(n) for n in ("y1_set", "z1_done", "y2_set", "z2_done"))
        x1T_set, gelu_done = sem("x1T_set"), sem("gelu_done")
        xb_set, x1_scaled, x1_done = sem("xb_set"), sem("x1_scaled"), sem("x1_done")
        fin_scaled, resid_set, fin_done = sem("fin_scaled"), sem("resid_set"), sem("fin_done")
        last_done = sem("last_done")

        STEPS = UNITS * CHUNKS
        ITEMS = [("q", 0, 0, 0), ("q", 0, 0, 1), ("k", 0), ("k", 1), ("v", 0), ("v", 1), ("q", 0, 1, 0), ("q", 0, 1, 1),
                 ("q", 1, 0, 0), ("q", 1, 0, 1), ("q", 1, 1, 0), ("q", 1, 1, 1)]
        SPLITS = [it for it in ITEMS if it[0] != "v"]
        bank_of = {it: n % 8 for n, it in enumerate(ITEMS)}
        ITEMS_FIRST = 6
        PROJECT_AT = (STEPS - 10, STEPS - 5)
        X1T_BANK = ((6, 6), (6, 7))
        N_Q = len(Q_PARTS) * 16
        G_KDMA = 16 * (KC * len(K_PARTS) + NB)

        def parts_of(item):
            if item[0] == "k":
                return ksp[:, item[1]]
            _, b, c, half = item
            return qsp[:, (2 * b + c) % 3, :, half * BLK:(half + 1) * BLK]

        USES = []
        for u in range(UNITS):
            for s_ in range(2 * QT):
                USES.append(("scores", u, s_ // 2, s_ % 2))
                if u and s_ == SPLIT_LAG - 1:
                    USES.append(("transpose", u - 1))
        USES.append(("transpose", UNITS - 1))
        use_of = {use: n for n, use in enumerate(USES)}

        def uses_before(g):
            if g > STEPS - LAST_STEPS:
                return len(USES)
            return min(LEAD_USES + -(-(2 * QT + 1) * g // CHUNKS), len(USES) - 1)

        def chunk_of(k):
            return k // 4, k % 2, k // 2 % 2

        ORDER = [("item", 8), ("item", 9), ("ada1",), ("item", 10), ("item", 11), ("uses", 2), ("ada2", 0), ("uses", 5),
                 ("ada2", 1), ("uses", 5), ("ada2", 2), ("uses", 5), ("ada2", 3), ("uses", 5), ("ada2", 4), ("uses", 3),
                 ("ada2", 5), ("uses", 3)]
        assert sum(o[1] for o in ORDER if o[0] == "uses") == LEAD_USES
        ADA2_BANKS = (7, 0, 1, 0, 1, 7)

        def walk(on_item, on_ada1, on_ada2, on_use):
            used = 0
            for what, *arg in ORDER:
                if what == "item":
                    on_item(arg[0])
                elif what == "ada1":
                    on_ada1()
                elif what == "ada2":
                    on_ada2(arg[0])
                else:
                    for _ in range(arg[0]):
                        on_use(used)
                        used += 1

        RECIP_AT = tuple(uses_before(16 * v + 25) for v in range(2))

        def nothing(*_):
            pass

        block = ctx.enter_context(nc.Block())


        def sp_wait(signal, value):
            nc.sync.wait_ge(signal, value)
            nc.sync.sem_inc(sp_passed, 1)

        def general_sp(sp, xv, k_rows, load_rows):
            xg = xTs[:, :, 0:NB * KB].rearrange("p k (b t) -> p k b t", b=NB)

            def project(k, kb):
                for b in range(NB):
                    sp.dma_start(xg[:, :, b, :], xv[:, :, b, bass.ds(kb * KB, KB)]).then_inc(g_x, 16)
                sp_wait(g_lo, k + 1)
                for c in range(KC):
                    k_rows(c, g_kdma)
                for b in range(NB):
                    sp.dma_start(kst[ONE_ROW:ONE_ROW + 1, :, b, :],
                                 mbias[0:1, b:b + 1, bass.ds(kb * KB, KB)].to_broadcast([1, H, KB])).then_inc(g_kdma, 16)
                sp_wait(g_kdma, G_KDMA * (k + 1))

            with sp.Fori(0, NKB) as kb:
                project(kb, kb)
                sp_wait(g_mx, 2 * QT * UNITS * kb + 2 * QT * UNITS)
            with sp.Fori(0, UNITS) as u:
                sp_wait(g_nmTe, u + 1)
                sp.dma_start(qst[MAX_ROW:ROWS, bass.ds(4 * u, 4), :], nmT[:, 0, :]).then_inc(g_mdma, 16)
                sp_wait(g_mdma, 16 * (u + 1))
            sp.wait_ge(g_zero, 1)
            with sp.Fori(0, UNITS) as u:
                sp.dma_start(ot_dram[bass.ds(u, 1), :, :].rearrange("o p t -> (o p) t"), ots[:, 0, :]).then_inc(g_zdma, 16)
                sp_wait(g_zdma, 16 * (u + 1))
            with sp.Fori(0, NKB) as kb:
                project(kb + NKB, kb)
                with sp.Fori(0, UNITS) as u:
                    row = ot_dram[bass.ds(u, 1), :, :].rearrange("o p t -> (o p) t")
                    sp.dma_start(ots[:, 0, :], row).then_inc(g_old, 16)
                    sp_wait(g_add, 2 * UNITS * kb + 2 * u + 2)
                    sp.dma_start(row, ots[:, 1, :]).then_inc(g_store, 16)
                    sp_wait(g_store, 16 * UNITS * kb + 16 * u + 16)
            with sp.Fori(0, 4) as v:
                load_rows(v, sp_wait)
                sp_wait(attn_ready, v + 1)

        def general_pe(pe, scores, scores_T, with_v):
            def project(k, with_values):
                pe.wait_ge(g_x, 32 * k + 32)
                xg = xTs[:, :, 0:NB * KB]
                for c in range(KC):
                    for kc in range(KC):
                        last = nc.tensor.matmul(PS[:, c, :], wqkvs[:, kc, C + P * c:C + P * (c + 1)], xg[:, kc, :],
                                                start=kc == 0, stop=kc == KC - 1)
                if with_values:
                    for b in range(NB):
                        for kt in range(KT):
                            for kc in range(KC):
                                last = nc.tensor.matmul(PS[:, 2 + b, kt * C:(kt + 1) * C],
                                                        xg[:, kc, KB * b + P * kt:KB * b + P * (kt + 1)],
                                                        wqkvs[:, kc, 2 * C:3 * C], start=kc == 0, stop=kc == KC - 1)
                last.then_inc(g_proj, 1)

            for v in range(4):
                pe.wait_ge(q_dma[v], N_Q)
            pe.wait_ge(red_done, LEAD_USES)
            pe.wait_ge(rest_done, len(SPLITS))
            pe.wait_ge(mods_raw, 6)
            with pe.Fori(0, NKB) as kb:
                project(kb, False)
                for b in range(NB):
                    with pe.Fori(0, 4) as g:
                        n = 2 * QT * UNITS * kb + 2 * QT * 4 * b + 2 * QT * g
                        pe.wait_ge(g_kdma, G_KDMA * kb + G_KDMA)
                        for qt in range(QT):
                            for pr in range(2):
                                if qt >= 1:
                                    pe.wait_ge(g_red, n + 2 * qt + pr - 1)
                                for i in range(2):
                                    last = scores(PS[:, 4 + pr, KB * i:KB * (i + 1)], b, g, 2 * pr + i, qt)
                                last.then_inc(g_mx, 1)
                        pe.wait_ge(g_red, n + 2 * QT)
            with pe.Fori(0, UNITS) as u:
                pe.wait_ge(g_nm, 5 * u + 5)
                nc.tensor.transpose(PS[0:96, 6, 0:P // 2].bitcast(BF16), nmsp[:, 0, :, :].rearrange("p s m -> p (s m)"),
                                    identb[:, :]).then_inc(g_nmT, 1)
            pe.wait_ge(g_mdma, 16 * UNITS)
            with pe.Fori(0, NKB) as kb:
                project(kb + NKB, True)
                for b in range(NB):
                    with pe.Fori(0, 4) as g:
                        u = g + 4 * b
                        n = CHUNKS * UNITS * kb + CHUNKS * u
                        pe.wait_ge(g_kdma, G_KDMA * (kb + NKB) + G_KDMA)
                        pe.wait_ge(g_vm, kb + 1)
                        pe.wait_ge(g_vu, UNITS * kb + u + 1)
                        for k in range(CHUNKS):
                            scores_T(k % 2, b, g, k).then_inc(g_st, 1)
                            pe.wait_ge(g_exp, n + k + 1)
                            with_v(k, lambda kt, h: vunit[:, kt, 32 * h:32 * (h + 1)]).then_inc(g_pv, 1)
                            if k % 4 == 3:
                                pe.wait_ge(g_add, 2 * UNITS * kb + 2 * u + k // 4 + 1)

        def general_dve(dve, split_maxima):
            def parts_of_k(k):
                dve.wait_ge(g_hi, k + 1)
                nc.vector.tensor_tensor(rest[:, :, :], PS[:, 0:2, :], ksp[:, :, 0, :], ALU.subtract).then_inc(g_rest, 1)
                dve.wait_ge(g_rest, k + 1)
                nc.vector.tensor_copy(ksp[:, :, 1, :], rest[:, :, :]).then_inc(g_mid, 1)
                dve.wait_ge(g_mid, k + 1)
                nc.vector.tensor_tensor(ksp[:, :, 2, :], rest[:, :, :], ksp[:, :, 1, :], ALU.subtract).then_inc(g_lo, 1)

            dve.wait_ge(nm_split, 5)
            nc.vector.memset(nmall[:, :, :], 3.0e38).then_inc(g_min, 1)
            with dve.Fori(0, NKB) as kb:
                parts_of_k(kb)
                with dve.Fori(0, UNITS) as u:
                    n = 2 * QT * UNITS * kb + 2 * QT * u
                    dve.wait_ge(g_min, UNITS * kb + u + 1)
                    for qt in range(QT):
                        for pr in range(2):
                            dve.wait_ge(g_mx, n + 2 * qt + pr + 1)
                            nc.vector.tensor_reduce(nmax[:, 0, 2 * pr:2 * pr + 2, qt],
                                                    PS[:, 4 + pr, :].rearrange("p (i t) -> p i t", i=2),
                                                    AX.X, ALU.max, negate=True).then_inc(g_red, 1)
                    dve.wait_ge(g_red, n + 2 * QT)
                    old = nmall[:, bass.ds(u, 1), :].rearrange("p o m -> p (o m)")
                    nc.vector.tensor_tensor(old, old, nmax[:, 0, :, :].rearrange("p i t -> p (i t)"), ALU.min).then_inc(g_min, 1)
            dve.wait_ge(g_min, NKB * UNITS + 1)
            with dve.Fori(0, UNITS) as u:
                split_maxima(dve, nc.vector, nmall[:, bass.ds(u, 1), :].rearrange("p o m -> p (o m)"), 0, g_nm, 5 * u)
                dve.wait_ge(g_nmT, u + 1)
                nc.vector.tensor_copy(nmT[:, 0, :], PS[0:96, 6, 0:P // 2].bitcast(BF16)).then_inc(g_nmTe, 1)
                dve.wait_ge(g_mdma, 16 * u + 16)
            nc.vector.memset(ots[:, 0, :], 0.0).then_inc(g_zero, 1)
            with dve.Fori(0, NKB) as kb:
                parts_of_k(kb + NKB)
                nc.vector.tensor_copy(maskb[:, :, :], maskc[:, :, bass.ds(kb * KT, KT)]).then_inc(g_vcol, 1)
                dve.wait_ge(g_vcol, kb + 1)
                for b in range(NB):
                    for kt in range(KT):
                        nc.vector.tensor_scalar(vaug[:, 4 * b:4 * (b + 1), kt, :, 0:D],
                                                PS[:, 2 + b, C * kt:C * (kt + 1)].rearrange("p (g i d) -> p g i d", i=4, d=D),
                                                maskb[:, b, kt:kt + 1], None, ALU.mult)
                        for g in range(4):
                            last = nc.vector.tensor_copy(vaug[:, 4 * b + g, kt, :, D:2 * D],
                                                         maskb[:, b, kt:kt + 1][:, :, None].to_broadcast([P, 4, D]))
                last.then_inc(g_vm, 1)
                with dve.Fori(0, UNITS) as u:
                    for half in range(2):
                        dve.wait_ge(g_pv, CHUNKS * UNITS * kb + CHUNKS * u + 4 * half + 4)
                        if half == 0:
                            dve.wait_ge(g_old, 16 * UNITS * kb + 16 * u + 16)
                        nc.vector.tensor_tensor(ots[:, 1, BLK * half:BLK * (half + 1)], PS[:, 7, :],
                                                ots[:, 0, BLK * half:BLK * (half + 1)], ALU.add).then_inc(g_add, 1)
        def reciprocal_of(dve, v):
            dve.wait_ge(den_dma, 16 * v + 16)
            nc.vector.reciprocal(denom[:, :], denom[:, :]).then_inc(recip_done, 1)

        def split_maxima(eng, ops, src, at, signal, base):
            rs = nmrest[:, at, :]
            ops.tensor_copy(nmsp[:, at, 0, :], src).then_inc(signal, 1)
            eng.wait_ge(signal, base + 1)
            ops.tensor_tensor(rs, src, nmsp[:, at, 0, :], ALU.subtract).then_inc(signal, 1)
            eng.wait_ge(signal, base + 2)
            ops.tensor_copy(nmsp[:, at, 1, :], rs).then_inc(signal, 1)
            eng.wait_ge(signal, base + 3)
            ops.tensor_tensor(rs, rs, nmsp[:, at, 1, :], ALU.subtract).then_inc(signal, 1)
            eng.wait_ge(signal, base + 4)
            ops.tensor_copy(nmsp[:, at, 2, :], rs).then_inc(signal, 1)

        @block.sync
        def _(sp):
            sp.dma_start(wqkvs[:, :, :], wqkv.rearrange("(k p) n -> p k n", p=P)).then_inc(w_loaded, 16)
            xv = xT.rearrange("(k p) t -> p k t", p=P)
            for i in (0, 1, 3, 2):
                sp.dma_start(xTs[:, :, i * BLK:(i + 1) * BLK], xv[:, :, i * BLK:(i + 1) * BLK]).then_inc(x_loaded[i], 16)
            sp.wait_ge(consts, 2)
            for b in range(NB):
                sp.dma_start(kst[ONE_ROW:ONE_ROW + 1, :, b, :],
                             mbias[0:1, b:b + 1, S - KB:S].to_broadcast([1, H, KB])).then_inc(rows_dma, 16)
            sp.dma_start(kst[MAX_ROW:ROWS, :, :, :],
                         ones[0:1, None, :].to_broadcast([1, (ROWS - MAX_ROW) * H * NB * KB // S, S])).then_inc(rows_dma, 16)
            sp.dma_start(qst[ONE_ROW:ONE_ROW + 1, :, :],
                         ones[0:1, None, :].to_broadcast([1, UNITS * 4, S])).then_inc(rows_dma, 16)

            def stack_q(b, c):
                sp.wait_ge(lo_done, SPLITS.index(("q", b, c, 1)) + 1)
                for n, part in enumerate(Q_PARTS):
                    sp.dma_start(qst[D * n:D * (n + 1), H * b + HC * c:H * b + HC * (c + 1), :],
                                 qsp[:, (2 * b + c) % 3, part, :]).then_inc(q_dma[2 * b + c], 16)

            def k_rows(c, signal):
                for n, part in enumerate(K_PARTS):
                    sp.dma_start(kst[D * n:D * (n + 1), HC * c:HC * (c + 1), :, :],
                                 ksp[:, c, part, :].rearrange("p (b t) -> p b t", b=NB)).then_inc(signal, 16)

            def stack_k(c):
                sp.wait_ge(lo_done, SPLITS.index(("k", c)) + 1)
                k_rows(c, k_dma[c])

            stack_q(0, 0)
            stack_k(0)
            stack_q(0, 1)
            stack_k(1)
            sp.dma_start(ba2s[:, :], ba2[None, :].to_broadcast([P, 6 * C])).then_inc(ba2_loaded, 16)
            stack_q(1, 0)
            stack_q(1, 1)

            def mlp_loads():
                sp.dma_start(wps[:, :, :], wp.rearrange("(k p) n -> p k n", p=P)).then_inc(mlp_loaded, 16)
                sp.dma_start(bps[:, :], bp[None, :].to_broadcast([P, C])).then_inc(mlp_loaded, 16)
                sp.dma_start(w1s[:, :, :], w1.rearrange("(k p) n -> p k n", p=P)).then_inc(mlp_loaded, 16)
                sp.dma_start(b1s[:, :], b1).then_inc(mlp_loaded, 16)
                sp.dma_start(w2s[:, :, :], w2.rearrange("(k p) n -> p k n", p=P)).then_inc(mlp_loaded, 16)
                sp.dma_start(b2s[:, :], b2[None, :].to_broadcast([P, C])).then_inc(mlp_loaded, 16)

            xd = x.rearrange("(t p) c -> p t c", p=P)
            od = out.rearrange("(t p) c -> p t c", p=P)

            def load_x(t):
                sp.dma_start(xb[t % 2][:, :, :], xd[:, 4 * t:4 * t + 4, :]).then_inc(xb_loaded[t % 2], 16)

            def stack_maxima(u):
                sp.wait_ge(red_done, use_of["transpose", u] + 1)
                sp.dma_start(qst[MAX_ROW:ROWS, 4 * u:4 * u + 4, :], nmT[:, u % 2, :]).then_inc(m_dma, 16)

            def rows_out(u):
                sp.wait_ge(ot_evac, 2 * u + 2)
                sp.dma_start(ot_dram[u, :, :], ots[:, u % 2, :]).then_inc(ot_dma[u % 2], 16)

            def load_rows(v, wait=sp.wait_ge):
                rows = ot_dram[bass.ds(2 * v, 2), :, :].rearrange("g (i r) t -> (g i) r t", r=2 * D)
                sp.dma_start(denom[:, :], rows[:, D, :].rearrange("h (s t) -> h s t", t=HC * S // P)).then_inc(den_dma, 16)
                sp.dma_start(numer[:, :], rows[:, 0:D, :]).then_inc(nd_dma, 16)
                wait(recip_done, v + 1)
                back = recip_dram[bass.ds(v, 1), :, :].rearrange("o h t -> (o h) t")
                sp.dma_start(back, denom[:, :]).then_inc(recip_dma, 16)
                wait(recip_dma, 16 * v + 16)
                sp.dma_start(recips[:, :], back[:, None, :].to_broadcast([HC, D, S])).then_inc(nd_dma, 16)

            with nc.sync.register("sp_flag") as r:
                sp.wait_ge(consts, 3)
                sp.reg_load(r, flag[0:1, 0:1])
                with sp.If_eq(r, 0):
                    stack_maxima(0)
                    mlp_loads()
                    stack_maxima(1)
                    for u in range(UNITS):
                        rows_out(u)
                        if u + 2 < UNITS:
                            stack_maxima(u + 2)
                        if u % 2 == 1:
                            for s_ in ot_dma:
                                sp.wait_ge(s_, 16 * (u // 2 + 1))
                            if u > 1:
                                sp.wait_ge(attn_ready, u // 2)
                            load_rows(u // 2)
                        if u == 3:
                            sp.wait_ge(st_done, CHUNKS * 4)
                            load_x(0)
                            load_x(1)
                with sp.If_ne(r, 0):
                    mlp_loads()
                    general_sp(sp, xT.rearrange("(k p) (b t) -> p k b t", p=P, b=NB), k_rows, load_rows)
                    load_x(0)
                    load_x(1)

            for t in range(4):
                if t < 2:
                    sp.wait_ge(x1_done, t + 1)
                    load_x(t + 2)
                if t < 3:
                    sp.wait_ge(fin_done, t + 1)
                    sp.dma_start(od[:, 4 * t:4 * t + 4, :], fin[t % 2][:, :, :]).then_inc(out_dma[t % 2], 16)
            for half in range(2):
                sp.wait_ge(last_done, half + 1)
                sp.dma_start(od[:, 12 + 2 * half:14 + 2 * half, :],
                             fin[1][:, 2 * half:2 * half + 2, :]).then_inc(out_dma[1], 16)
            sp.wait_ge(out_dma[0], 32)
            sp.wait_ge(out_dma[1], 48)

        @block.gpsimd
        def _(pool):
            pool.wait_ge(consts, 4)
            for b in range(NB):
                for kt in range(KT):
                    col = maskc[:, b, QT - KT + kt:QT - KT + kt + 1]
                    last = nc.gpsimd.tensor_copy(vaug[:, 4 * b:4 * (b + 1), kt, :, D:2 * D],
                                                 col[:, :, None, None].to_broadcast([P, 4, 4, D]))
            last.then_inc(vmask_done, 1)

            def low_parts(n):
                pool.wait_ge(mid_done, n + 1)
                parts = parts_of(SPLITS[n])
                nc.gpsimd.tensor_tensor(parts[:, 2, :], rest[:, n % 2, :], parts[:, 1, :], ALU.subtract).then_inc(lo_done, 1)

            def add_bias(n):
                b, part = n // 3, n % 3
                pool.wait_ge(ba2_loaded, 16)
                pool.wait_ge(mods_raw, n + 1)
                m = mods[:, b, 2 * part:2 * part + 2, :].rearrange("p m c -> p (m c)")
                nc.gpsimd.tensor_tensor(m, m, ba2s[:, BLK * part:BLK * (part + 1)], ALU.add).then_inc(mods_set, 1)

            def split(u):
                at = u % 2
                pool.wait_ge(red_done, use_of["scores", u, QT - 1, 1] + 1)
                if u >= 2:
                    pool.wait_ge(mx_done, use_of["transpose", u - 2] + 1)
                split_maxima(pool, nc.gpsimd, nmax[:, at, :, :].rearrange("p i t -> p (i t)"), at, nm_split, 5 * u)

            for n in range(ITEMS_FIRST):
                low_parts(n)
            walk(lambda n: low_parts(SPLITS.index(ITEMS[n])), nothing, add_bias,
                 lambda n: split(0) if USES[n] == ("scores", 0, QT - 1, 1) else None)

            def fold():
                pool.wait_ge(mods_set, 6)
                for h0 in (0, 3):
                    gate = mods[:, :, h0 + 2, :]
                    nc.gpsimd.tensor_tensor(mods[:, :, h0, :], mods[:, :, h0, :], gate, ALU.mult)
                    nc.gpsimd.tensor_tensor(mods[:, :, h0 + 1, :], mods[:, :, h0 + 1, :], gate, ALU.mult).then_inc(mods_set, 1)
                pool.wait_ge(mods_set, 8)
                for h0 in (0, 3):
                    gate = mods[:, :, h0 + 2, :]
                    nc.gpsimd.tensor_tensor(mods[:, :, h0 + 1, :], mods[:, :, h0 + 1, :], gate, ALU.add).then_inc(mods_set, 1)

            def normalise(v, n):
                pool.wait_ge(nd_dma, 32 * n)
                nc.gpsimd.tensor_tensor(attn[:, bass.ds(v, 1), :].rearrange("p o t -> p (o t)"),
                                        numer[:, :], recips[:, :], ALU.mult).then_inc(attn_ready, 1)

            def block_x1(t):
                b = t // 2
                if t == 0:
                    pool.wait_ge(mods_set, 10)
                pool.wait_ge(xb_loaded[t % 2], 16 * (t // 2 + 1))
                nc.gpsimd.tensor_tensor(xb[t % 2][:, :, :], xb[t % 2][:, :, :],
                                        mods[:, b, 0:1, :].to_broadcast([P, 4, C]), ALU.add).then_inc(xb_set, 1)
                pool.wait_ge(z1_done, t + 1)
                if t >= 2:
                    pool.wait_ge(resid_set, t - 1)
                nc.gpsimd.tensor_tensor(x1[t % 2][:, :, :], y1[:, :, :],
                                        mods[:, b, 1:2, :].to_broadcast([P, 4, C]), ALU.mult).then_inc(x1_scaled, 1)
                pool.wait_ge(xb_set, t + 1)
                pool.wait_ge(x1_scaled, t + 1)
                nc.gpsimd.tensor_tensor(x1[t % 2][:, :, :], x1[t % 2][:, :, :], xb[t % 2][:, :, :],
                                        ALU.add).then_inc(x1_done, 1)

            pool.wait_ge(v_evac, NB * KT)
            with nc.gpsimd.register("pool_flag") as r:
                pool.reg_load(r, flag[0:1, 0:1])
                with pool.If_eq(r, 0):
                    split(1)
                    fold()
                    split(2)
                    split(3)
                    for v in range(2):
                        split(2 * v + 4)
                        normalise(v, v + 1)
                        split(2 * v + 5)
                    normalise(2, 3)
                    block_x1(0)
                    block_x1(1)
                    normalise(3, 4)
                with pool.If_ne(r, 0):
                    fold()
                    with pool.Fori(0, NKB) as kb:
                        with pool.Fori(0, UNITS) as u:
                            pool.wait_ge(g_vm, kb + 1)
                            src = vaug[:, bass.ds(u, 1), :, :, :].rearrange("p o k i d -> p (o k) (i d)")
                            nc.gpsimd.tensor_copy(vunit[:, :, :], src).then_inc(g_vu, 1)
                            pool.wait_ge(g_pv, CHUNKS * UNITS * kb + CHUNKS * u + CHUNKS)
                    with pool.Fori(0, 4) as v:
                        normalise(v, v + 1)
                    block_x1(0)
                    block_x1(1)

            def residual(t):
                if t == 0:
                    pool.wait_ge(lo_done, len(SPLITS))
                if t >= 2:
                    pool.wait_ge(fin_done, t - 1)
                pool.wait_ge(x1_done, t + 1)
                nc.gpsimd.tensor_tensor(resid[t % 2][:, :, :], x1[t % 2][:, :, :],
                                        mods[:, t // 2, 3:4, :].to_broadcast([P, 4, C]), ALU.add).then_inc(resid_set, 1)

            def finish(t):
                pool.wait_ge(z2_done, t + 1)
                if t >= 2:
                    pool.wait_ge(out_dma[t % 2], 16)
                nc.gpsimd.tensor_tensor(fin[t % 2][:, :, :], y2[:, :, :],
                                        mods[:, t // 2, 4:5, :].to_broadcast([P, 4, C]), ALU.mult).then_inc(fin_scaled, 1)
                pool.wait_ge(fin_scaled, t + 1)
                pool.wait_ge(resid_set, t + 1)
                nc.gpsimd.tensor_tensor(fin[t % 2][:, :, :], fin[t % 2][:, :, :], resid[t % 2][:, :, :],
                                        ALU.add).then_inc(fin_done, 1)

            residual(0)
            residual(1)
            for t in range(2, 4):
                block_x1(t)
                finish(t - 2)
                residual(t)
            finish(2)

        @block.tensor
        def _(pe):
            pe.wait_ge(w_loaded, 16)
            keys = xTs[:, :, :].rearrange("p k (b t) -> p k b t", b=NB)[:, :, :, S - KB:S]

            def item(n):
                it = ITEMS[n]
                if n >= 8:
                    pe.wait_ge(rest_done, SPLITS.index(ITEMS[n - 8]) + 1)
                bank = PS[:, n % 8, :]
                for k in range(KC):
                    if it[0] == "q":
                        _, b, c, half = it
                        pe.wait_ge(x_loaded[2 * b + half], 16)
                        last = nc.tensor.matmul(bank, wqkvs[:, k, P * c:P * (c + 1)],
                                                xTs[:, k, b * S + half * BLK:b * S + (half + 1) * BLK],
                                                start=k == 0, stop=k == KC - 1)
                    elif it[0] == "k":
                        c = it[1]
                        pe.wait_ge(x_loaded[1], 16)
                        pe.wait_ge(x_loaded[3], 16)
                        last = nc.tensor.matmul(bank.rearrange("p (b t) -> p b t", b=NB),
                                                wqkvs[:, k, C + P * c:C + P * (c + 1)],
                                                keys[:, k, :, :], start=k == 0, stop=k == KC - 1)
                if it[0] == "v":
                    b = it[1]
                    for kt in range(KT):
                        for k in range(KC):
                            last = nc.tensor.matmul(bank[:, kt * C:(kt + 1) * C], keys[:, k, b, P * kt:P * (kt + 1)],
                                                    wqkvs[:, k, 2 * C:3 * C], start=k == 0, stop=k == KC - 1)
                last.then_inc(v_done if it[0] == "v" else proj_done, 1)

            def ada1():
                pe.wait_ge(ada_loaded, 16 * 3)
                pe.wait_ge(rest_done, SPLITS.index(ITEMS[7]) + 1)
                for m in range(KC):
                    for k in range(KC):
                        last = nc.tensor.matmul(PS[:, 7, NB * m:NB * (m + 1)], wa1s[:, k, P * m:P * (m + 1)],
                                                cTs[:, k, :], start=k == 0, stop=k == KC - 1)
                last.then_inc(ada1_done, 1)

            def ada2(n):
                b, part = n // 3, n % 3
                bank = ADA2_BANKS[n]
                if n == 0:
                    pe.wait_ge(ada2_loaded, 16)
                    pe.wait_ge(dve_step, 4)
                if bank in ADA2_BANKS[:n]:
                    pe.wait_ge(mods_raw, ADA2_BANKS[:n].index(bank) + 1)
                elif bank < 2:
                    pe.wait_ge(rest_done, SPLITS.index(ITEMS[8 + bank]) + 1)
                for k in range(KC):
                    last = nc.tensor.matmul(PS[:, bank, :], sil[:, 2, NB * k + b:NB * k + b + 1].to_broadcast([P, P]),
                                            wa2s[:, k, BLK * part:BLK * (part + 1)], start=k == 0, stop=k == KC - 1)
                last.then_inc(ada2_done, 1)

            def at_head(ap, h):
                return ap[:, bass.ds(h, 1), :].rearrange("p o t -> p (o t)")

            def scores(bank, b, g, i, tile):
                return nc.tensor.matmul(bank, at_head(qst[0:MAX_ROW, :, P * tile:P * (tile + 1)], 16 * b + 4 * g + i),
                                        at_head(kst[0:MAX_ROW, :, b, :], 4 * g + i), start=True, stop=True)

            def scores_T(slot_, b, g, k):
                half, pr, kt = chunk_of(k)
                for i in range(2 * pr, 2 * pr + 2):
                    last = nc.tensor.matmul(PS[:, 2 * slot_ + i % 2, :],
                                            at_head(kst[0:ROWS, :, b, P * kt:P * (kt + 1)], 4 * g + i),
                                            at_head(qst[0:ROWS, :, BLK * half:BLK * (half + 1)], 16 * b + 4 * g + i),
                                            start=True, stop=True)
                return last

            def with_v(k, v_of):
                half, pr, kt = chunk_of(k)
                for i in range(2):
                    h = 2 * pr + i
                    last = nc.tensor.matmul(PS[32 * h:32 * (h + 1), 7, :], v_of(kt, h),
                                            probs[:, k % 4, i, :], start=kt == 0, stop=kt == KT - 1, tile_position=(0, 32 * h))
                return last

            def use(n):
                what, u, *rest_ = USES[n]
                if n == 0:
                    pe.wait_ge(v_evac, NB * KT)
                    pe.wait_ge(rest_done, SPLITS.index(ITEMS[6]) + 1)
                    pe.wait_ge(rows_dma, 64)
                if n >= 3:
                    pe.wait_ge(red_done, n - 2)
                if what == "transpose":
                    pe.wait_ge(nm_split, 5 * u + 5)
                    if u == 0:
                        pe.wait_ge(consts, 5)
                    last = nc.tensor.transpose(PS[0:96, 4 + n % 3, 0:P // 2].bitcast(BF16),
                                               nmsp[:, u % 2, :, :].rearrange("p s m -> p (s m)"), identb[:, :])
                else:
                    qt, pr = rest_
                    if u % 2 == 0 and qt == 0 and pr == 0:
                        pe.wait_ge(q_dma[u // 2], N_Q)
                        if u < 4:
                            pe.wait_ge(k_dma[u // 2], 16 * len(K_PARTS))
                    for i in range(2):
                        last = scores(PS[:, 4 + n % 3, KB * i:KB * (i + 1)], u // 4, u % 4, 2 * pr + i, qt)
                last.then_inc(mx_done, 1)

            def project_tile(t, tile):
                if t == 0 and tile == 0:
                    pe.wait_ge(mlp_loaded, 16 * 6)
                if tile == 0:
                    pe.wait_ge(attn_ready, 2 * (t // 2) + 2)
                if tile % 2 == 0 and t >= 1:
                    pe.wait_ge(y1_set, 2 * t - 1 + tile // 2)
                at = BLK * (t % 2) + P * tile
                for c in range(KC):
                    last = nc.tensor.matmul(PS[:, 4 + tile // 2, C * (tile % 2):C * (tile % 2 + 1)],
                                            attn[:, 2 * (t // 2) + c, at:at + P], wps[:, c, :],
                                            start=c == 0, stop=c == KC - 1)
                if tile % 2:
                    last.then_inc(y1_mm, 1)

            def transpose_x1(t, c):
                if c == 0:
                    pe.wait_ge(x1_done, t + 1)
                if t == 0 and c == 1:
                    pe.wait_ge(x1T_set, 1)
                elif t >= 1:
                    pe.wait_ge(x1T_set, 2 * t)
                for tile in range(4):
                    last = nc.tensor.transpose(PS[:, X1T_BANK[min(t, 1)][c], P * tile:P * (tile + 1)],
                                               x1[t % 2][:, tile, P * c:P * (c + 1)], identf[:, :])
                last.then_inc(x1T_mm, 1)

            def products(g):
                u, k = g // CHUNKS, g % CHUNKS
                pe.wait_ge(exp_done, g + 2)
                if g == 0:
                    pe.wait_ge(vmask_done, 1)
                    pe.wait_ge(mods_raw, 6)
                if g % 4 == 0 and g:
                    pe.wait_ge(ot_evac, g // 4)
                for k_ in (k, k + 1):
                    last = with_v(k_, lambda kt, h: vaug[:, u, kt, h, :])
                last.then_inc(pv_done, 1)

            def chunk(g):
                u, k = g // CHUNKS, g % CHUNKS
                uses = range(uses_before(g), uses_before(g + 1))
                if g == 0:
                    pe.wait_ge(rest_done, len(SPLITS))
                    pe.wait_ge(mods_raw, 5)
                if k == 0:
                    pe.wait_ge(m_dma, 16 * u + 16)
                if g >= 2:
                    pe.wait_ge(exp_done, g - 1)
                scores_T(k % 2, u // 4, u % 4, k).then_inc(st_done, 1)
                for n in uses[:1]:
                    use(n)
                if g and g % 2 == 0:
                    products(g - 2)
                for n in uses[1:]:
                    use(n)
                for t in range(2):
                    if 0 <= g - PROJECT_AT[t] < 4:
                        if g == PROJECT_AT[0]:
                            pe.wait_ge(red_done, len(USES))
                        project_tile(t, g - PROJECT_AT[t])
                if g >= STEPS - 2:
                    transpose_x1(0, g - (STEPS - 2))

            for n in range(8):
                item(n)
            walk(item, ada1, ada2, use)
            with nc.tensor.register("pe_flag") as r:
                pe.wait_ge(consts, 3)
                pe.reg_load(r, flag[0:1, 0:1])
                with pe.If_eq(r, 0):
                    for g in range(STEPS):
                        chunk(g)
                    products(STEPS - 2)
                with pe.If_ne(r, 0):
                    general_pe(pe, scores, scores_T, with_v)
                    for t in range(2):
                        for tile in range(4):
                            project_tile(t, tile)
                    for c in range(KC):
                        transpose_x1(0, c)

            def fc1(t):
                pe.wait_ge(x1T_set, 2 * t + 2)
                for f in range(FF // P):
                    n = FF // P * t + f
                    if n >= 2:
                        pe.wait_ge(gelu_done, n - 1)
                    for c in range(KC):
                        last = nc.tensor.matmul(PS[:, f % 2, :], w1s[:, c, P * f:P * (f + 1)], x1T[t % 2][:, c, :],
                                                start=c == 0, stop=c == KC - 1)
                    last.then_inc(fc1_mm, 1)

            def fc2(t):
                for tile in range(4):
                    if tile % 2 == 0 and t >= 1:
                        pe.wait_ge(y2_set, 2 * t - 1 + tile // 2)
                    for f in range(FF // P):
                        pe.wait_ge(gelu_done, FF // P * t + f + 1)
                        last = nc.tensor.matmul(PS[:, 2 + tile // 2, C * (tile % 2):C * (tile % 2 + 1)],
                                                hid[t % 2][:, f, P * tile:P * (tile + 1)], w2s[:, f, :],
                                                start=f == 0, stop=f == FF // P - 1)
                    if tile % 2:
                        last.then_inc(fc2_mm, 1)

            for t in range(4):
                fc1(t)
                if t < 3:
                    for c in range(KC):
                        transpose_x1(t + 1, c)
                if t < 2:
                    for tile in range(4):
                        project_tile(t + 2, tile)
                fc2(t)

        @block.scalar
        def _(act):
            act.dma_start(mrow8[0:1, :, :], mask.rearrange("(o b) s -> o b s", o=1)).then_inc(mask_loaded, 16)
            act.dma_start(mask8[:, :], mask_cols).then_inc(mask_loaded, 16)
            act.dma_start(identf[:, :], ident).then_inc(mask_loaded, 16)
            act.dma_start(cTs[:, :, :], cT.rearrange("(k p) b -> p k b", p=P)).then_inc(ada_loaded, 16)
            act.dma_start(wa1s[:, :, :], wa1.rearrange("(k p) n -> p k n", p=P)).then_inc(ada_loaded, 16)
            act.dma_start(ba1s[:, :], ba1).then_inc(ada_loaded, 16)

            def from_bank(n):
                it = ITEMS[n]
                if it[0] == "v":
                    b = it[1]
                    act.wait_ge(v_done, b + 1)
                    act.wait_ge(consts, 4)
                    for kt in range(KT):
                        nc.scalar.activation(vaug[:, 4 * b:4 * (b + 1), kt, :, 0:D],
                                             PS[:, bank_of[it], C * kt:C * (kt + 1)].rearrange("p (g i d) -> p g i d", i=4, d=D),
                                             ACT.Copy, scale=maskc[:, b, QT - KT + kt:QT - KT + kt + 1]).then_inc(v_evac, 1)
                    return
                act.wait_ge(proj_done, SPLITS.index(it) + 1)
                if it[:3] == ("q", 1, 1):
                    act.wait_ge(q_dma[0], N_Q)
                nc.scalar.copy(parts_of(it)[:, 0, :], PS[:, bank_of[it], :]).then_inc(hi_done, 1)

            def silu_exp():
                act.wait_ge(dve_step, 1)
                nc.scalar.activation(sil[:, 1, :], sil[:, 0, :], ACT.Exp, scale=-1.0).then_inc(sil_exp, 1)

            def ada_out(n):
                b, part = n // 3, n % 3
                act.wait_ge(ada2_done, n + 1)
                nc.scalar.copy(mods[:, b, 2 * part:2 * part + 2, :].rearrange("p m c -> p (m c)"),
                               PS[:, ADA2_BANKS[n], :]).then_inc(mods_raw, 1)

            from_bank(0)
            act.dma_start(wa2s[:, :, :], wa2.rearrange("(k p) n -> p k n", p=P)).then_inc(ada2_loaded, 16)
            for n in range(1, 8):
                from_bank(n)
            walk(from_bank, silu_exp, ada_out, nothing)

            def exps(slot_, k, signal):
                nc.scalar.activation(probs[:, k % 4, :, :], PS[:, 2 * slot_:2 * slot_ + 2, :], ACT.Exp,
                                     scale=float(D) ** -0.5).then_inc(signal, 1)

            def rows_out(q):
                u, half = q // 2, q % 2
                act.wait_ge(pv_done, 2 * q + 2)
                if half == 0 and u >= 2:
                    act.wait_ge(ot_dma[u % 2], 16 * (u // 2))
                nc.scalar.copy(ots[:, u % 2, BLK * half:BLK * (half + 1)], PS[:, 7, :]).then_inc(ot_evac, 1)

            def x1T_out(t, c):
                act.wait_ge(x1T_mm, 2 * t + c + 1)
                nc.scalar.copy(x1T[t % 2][:, c, :], PS[:, X1T_BANK[min(t, 1)][c], :]).then_inc(x1T_set, 1)

            with nc.scalar.register("act_flag") as r:
                act.wait_ge(consts, 3)
                act.reg_load(r, flag[0:1, 0:1])
                with act.If_eq(r, 0):
                    for g in range(STEPS):
                        act.wait_ge(st_done, g + 1)
                        if g >= 4:
                            act.wait_ge(pv_done, (g - 4) // 2 + 1)
                        exps(g % 2, g, exp_done)
                        if g % 4 == 0 and g:
                            rows_out(g // 4 - 1)
                        if g >= STEPS - 2:
                            x1T_out(0, g - (STEPS - 2))
                    rows_out(STEPS // 4 - 1)
                with act.If_ne(r, 0):
                    def high_parts(k):
                        act.wait_ge(g_proj, k + 1)
                        nc.scalar.copy(ksp[:, :, 0, :], PS[:, 0:2, :]).then_inc(g_hi, 1)

                    with act.Fori(0, NKB) as kb:
                        high_parts(kb)
                    with act.Fori(0, NKB) as kb:
                        high_parts(kb + NKB)
                        with act.Fori(0, UNITS) as u:
                            n = CHUNKS * UNITS * kb + CHUNKS * u
                            for k in range(CHUNKS):
                                act.wait_ge(g_st, n + k + 1)
                                exps(k % 2, k, g_exp)
                                act.wait_ge(g_pv, n + k + 1)
                    for c in range(KC):
                        x1T_out(0, c)

            act.wait_ge(mlp_loaded, 16 * 6)

            for t in range(4):
                for f in range(FF // P):
                    act.wait_ge(fc1_mm, FF // P * t + f + 1)
                    if t >= 2 and f == 0:
                        act.wait_ge(fc2_mm, 2 * t - 2)
                    nc.scalar.activation(hid[t % 2][:, f, :], PS[:, f % 2, :], ACT.Gelu,
                                         bias=b1s[:, f:f + 1]).then_inc(gelu_done, 1)
                if t < 3:
                    for c in range(KC):
                        x1T_out(t + 1, c)

        @block.vector
        def _(dve):
            steps = [0]

            def step(ins):
                steps[0] += 1
                ins.then_inc(dve_step, 1)
                dve.wait_ge(dve_step, steps[0])

            dve.wait_ge(mask_loaded, 48)
            nc.vector.tensor_scalar(mbias[0:1, :, :], mrow8[0:1, :, :], MASKED, -MASKED, ALU.mult, ALU.add).then_inc(consts, 1)
            nc.vector.memset(ones[0:1, :], 1.0).then_inc(consts, 1)
            nc.vector.tensor_reduce(flagf[0:1, :], mrow8[0:1, :, 0:S - KEYS_FAST], AX.XY, ALU.max).then_inc(flag_step, 1)
            dve.wait_ge(flag_step, 1)
            nc.vector.tensor_copy(flag[0:1, :], flagf[0:1, :]).then_inc(consts, 1)
            nc.vector.tensor_copy(maskc[:, :, :], mask8[:, :].rearrange("p (b t) -> p b t", b=NB)).then_inc(consts, 1)
            nc.vector.tensor_copy(identb[:, :], identf[:, :]).then_inc(consts, 1)

            def rest_of(n):
                it = SPLITS[n]
                parts = parts_of(it)
                dve.wait_ge(hi_done, n + 1)
                if n >= 2:
                    dve.wait_ge(lo_done, n - 1)
                nc.vector.tensor_tensor(rest[:, n % 2, :], PS[:, bank_of[it], :], parts[:, 0, :],
                                        ALU.subtract).then_inc(rest_done, 1)
                dve.wait_ge(rest_done, n + 1)
                nc.vector.tensor_copy(parts[:, 1, :], rest[:, n % 2, :]).then_inc(mid_done, 1)

            def silu():
                dve.wait_ge(ada1_done, 1)
                dve.wait_ge(ada_loaded, 16 * 3)
                step(nc.vector.tensor_tensor(sil[:, 0, :].rearrange("p (k b) -> p k b", b=NB),
                                             PS[:, 7, 0:KC * NB].rearrange("p (k b) -> p k b", b=NB),
                                             ba1s[:, :, None].to_broadcast([P, KC, NB]), ALU.add))
                dve.wait_ge(sil_exp, 1)
                step(nc.vector.tensor_scalar_add(sil[:, 1, :], sil[:, 1, :], 1.0))
                step(nc.vector.reciprocal(sil[:, 1, :], sil[:, 1, :]))
                step(nc.vector.tensor_tensor(sil[:, 2, :], sil[:, 0, :], sil[:, 1, :], ALU.mult))

            def read_use(n):
                what, u, *where = USES[n]
                dve.wait_ge(mx_done, n + 1)
                if what == "transpose":
                    if u >= 2:
                        dve.wait_ge(m_dma, 16 * (u - 1))
                    nc.vector.tensor_copy(nmT[:, u % 2, :], PS[0:96, 4 + n % 3, 0:P // 2].bitcast(BF16)).then_inc(red_done, 1)
                else:
                    qt, pr = where
                    if u >= 2 and qt == 0 and pr == 0:
                        dve.wait_ge(nm_split, 5 * (u - 1))
                    nc.vector.tensor_reduce(nmax[:, u % 2, 2 * pr:2 * pr + 2, qt],
                                            PS[:, 4 + n % 3, :].rearrange("p (i t) -> p i t", i=2),
                                            AX.X, ALU.max, negate=True).then_inc(red_done, 1)

            for n in range(ITEMS_FIRST):
                rest_of(n)
            walk(lambda n: rest_of(SPLITS.index(ITEMS[n])), silu, nothing, read_use)

            def norm(t, half, banks, y, bias, mm, y_set, z_done, used, tiles=range(4)):
                if t >= 1 and 0 in tiles:
                    dve.wait_ge(used, t)
                part = slice(tiles[0], tiles[-1] + 1)
                for i in range(tiles[0] // 2, tiles[-1] // 2 + 1):
                    dve.wait_ge(mm, 2 * t + i + 1)
                    nc.vector.tensor_tensor(y[:, 2 * i:2 * i + 2, :],
                                            PS[:, banks + i, :].rearrange("p (t c) -> p t c", t=2),
                                            bias[:, None, :].to_broadcast([P, 2, C]), ALU.add).then_inc(y_set, 1)
                dve.wait_ge(y_set, 2 * t + tiles[-1] // 2 + 1)
                for i in tiles:
                    ins = nc.vector.bn_stats(stats[:, i, :], y[:, i, :])
                step(ins)
                for i in tiles:
                    ins = nc.vector.bn_aggr(mv[:, half, i, :], stats[:, i, :])
                step(ins)
                var, g, w, a = mv[:, half, part, 1], nwt[:, 0, part], nwt[:, 1, part], nwt[:, 2, part]
                step(nc.vector.tensor_scalar_add(a, var, EPS))
                step(nc.vector.tensor_scalar(w, a, -0.5, None, ALU.mult))
                step(nc.vector.tensor_single_scalar(nwt[:, 3, part].bitcast(I32), a.bitcast(I32), 1, ALU.logical_shift_right))
                step(nc.vector.tensor_scalar(g.bitcast(I32), nwt[:, 3, part].bitcast(I32), -1.0, float(0x5F3759DF), ALU.mult, ALU.add))
                for _ in range(3):
                    step(nc.vector.tensor_tensor(a, g, g, ALU.mult))
                    step(nc.vector.tensor_tensor(a, a, w, ALU.mult))
                    step(nc.vector.scalar_tensor_tensor(g, a, 1.5, g, ALU.add, ALU.mult))
                for i in tiles:
                    ins = nc.vector.tensor_scalar(y[:, i, :], y[:, i, :], mv[:, half, i, 0:1], nwt[:, 0, i:i + 1],
                                                  ALU.subtract, ALU.mult)
                ins.then_inc(z_done, 1)

            def norm1(t):
                if t == 0:
                    dve.wait_ge(mlp_loaded, 16 * 6)
                norm(t, 0, 4, y1, bps, y1_mm, y1_set, z1_done, x1_scaled)

            def norm2(t):
                norm(t, 1, 2, y2, b2s, fc2_mm, y2_set, z2_done, fin_scaled)

            with nc.vector.register("dve_flag") as r:
                dve.wait_ge(consts, 3)
                dve.reg_load(r, flag[0:1, 0:1])
                before = steps[0]
                with dve.If_eq(r, 0):
                    for n in range(LEAD_USES, len(USES)):
                        if n in RECIP_AT:
                            reciprocal_of(dve, RECIP_AT.index(n))
                        read_use(n)
                    reciprocal_of(dve, 2)
                    norm1(0)
                    norm1(1)
                    reciprocal_of(dve, 3)
                with dve.If_ne(r, 0):
                    steps[0] = before
                    general_dve(dve, split_maxima)
                    with dve.Fori(0, 4) as v:
                        reciprocal_of(dve, v)
                    norm1(0)
                    norm1(1)
            for t in range(3):
                if t < 2:
                    norm1(t + 2)
                norm2(t)

            t = 3
            dve.wait_ge(out_dma[t % 2], 16)
            for half in range(2):
                tiles = range(2 * half, 2 * half + 2)
                part = slice(2 * half, 2 * half + 2)
                norm(t, 1, 2, y2, b2s, fc2_mm, y2_set, z2_done, fin_scaled, tiles)
                dve.wait_ge(z2_done, t + half + 1)
                step(nc.vector.tensor_tensor(y2[:, part, :], y2[:, part, :],
                                             mods[:, t // 2, 4:5, :].to_broadcast([P, 2, C]), ALU.mult))
                dve.wait_ge(resid_set, t + 1)
                nc.vector.tensor_tensor(fin[t % 2][:, part, :], y2[:, part, :], resid[t % 2][:, part, :],
                                        ALU.add).then_inc(last_done, 1)

INPUTS = ("xT", "x", "cT", "mask", "mask_cols", "ident", "wqkv", "wp", "bp", "w1", "b1", "w2", "b2", "wa1", "ba1", "wa2", "ba2")


def kernel(x, cond_1024, mask_BxS_bk0, L0_cond_qkv_w, L0_cond_proj_w, L0_cond_proj_b, L0_cond_fc1_w, L0_cond_fc1_b,
           L0_cond_fc2_w, L0_cond_fc2_b, L0_cond_ada1_w, L0_cond_ada1_b, L0_cond_ada2_w, L0_cond_ada2_b):
    import concourse.bacc as bacc
    from concourse.bass_utils import run_bass_kernel_spmd

    tokens = np.asarray(x).reshape(T, C)
    mask = np.asarray(mask_BxS_bk0)
    qkv = np.asarray(L0_cond_qkv_w)
    qk = qkv[:, :2 * C].reshape(C, 2, KC, HC, D).transpose(0, 1, 2, 4, 3).reshape(C, 2 * C)
    arrays = {
        "xT": tokens.T, "x": tokens, "cT": np.asarray(cond_1024).T, "mask": mask,
        "mask_cols": mask.reshape(NB * QT, P).T, "ident": np.eye(P, dtype=np.float32),
        "wqkv": np.concatenate([qk, qkv[:, 2 * C:]], axis=1), "wp": L0_cond_proj_w, "bp": L0_cond_proj_b,
        "w1": L0_cond_fc1_w, "b1": np.asarray(L0_cond_fc1_b).reshape(FF // P, P).T, "w2": L0_cond_fc2_w, "b2": L0_cond_fc2_b,
        "wa1": L0_cond_ada1_w, "ba1": np.asarray(L0_cond_ada1_b).reshape(KC, P).T, "wa2": L0_cond_ada2_w, "ba2": L0_cond_ada2_b,
    }
    arrays = {n: np.ascontiguousarray(a) for n, a in arrays.items()}
    nc = bacc.Bacc("TRN2", target_bir_lowering=False, num_devices=1)
    aps = [nc.dram_tensor(f"in_{n}", arrays[n].shape, mybir.dt.from_np(arrays[n].dtype), kind="ExternalInput").ap()
           for n in INPUTS]
    result = nc.dram_tensor("result", (T, C), F32, kind="ExternalOutput").ap()
    cond_block(nc, *aps, result)
    r = run_bass_kernel_spmd(nc, [{f"in_{n}": a for n, a in arrays.items()}], core_ids=[0])
    return r.results[0]["result"].reshape(NB, S, C)
```

```python
from contextlib import ExitStack

import numpy as np

import concourse.bass as bass
from concourse import mybir

F32 = mybir.dt.float32
BF16 = mybir.dt.bfloat16
F32R = mybir.dt.float32r
I32 = mybir.dt.int32
U8 = mybir.dt.uint8
ALU = mybir.AluOpType
ACT = mybir.ActivationFunctionType
AX = mybir.AxisListType

NB, S, C, H = 2, 1024, 256, 16
D = C // H
FF = 4 * C
EPS = 1e-5
P = 128
KC = C // P
HC = P // D
T = NB * S
BLK = 512
KB = 256
NKB = S // KB
KEYS_FAST = KB
KT = KB // P
UNITS = NB * H // 4
QT = S // P
CHUNKS = 8
ROWS = 100
ONE_ROW, MAX_ROW = 96, 97
LEAD_USES = 26
FASTER = 4
WARM_UP = 9
SPLIT_LAG = 4
LAST_STEPS = 11
MASKED = 1.0e30
Q_PARTS = (0, 1, 2, 0, 1, 0)
K_PARTS = (0, 0, 0, 1, 1, 2)


def cond_block(nc, xT, x, cT, mask, mask_cols, ident, wqkv, wp, bp, w1, b1, w2, b2, wa1, ba1, wa2, ba2, out):
    mods_dram = nc.dram_tensor("modulation", (NB, 6 * C), F32, kind="Internal").ap()
    recip_dram = nc.dram_tensor("reciprocals", (4, HC, S), F32, kind="Internal").ap()
    ot_dram = nc.dram_tensor("attention_rows", (UNITS, P, S), F32, kind="Internal").ap()
    with ExitStack() as ctx:
        def sb(name, shape, dt):
            return ctx.enter_context(nc.sbuf_tensor(name, shape, dt))

        def sem(name):
            return ctx.enter_context(nc.semaphore(name))

        def view(region, at, shape, dt=F32):
            size = int(np.prod(shape)) * (1 if dt == F32 else 0.5)
            v = region[:, at:at + int(size)]
            if dt != F32:
                v = v.bitcast(dt)
            names = "abcd"[:len(shape)]
            if len(shape) > 1:
                v = v.rearrange(f"p ({' '.join(names)}) -> p {' '.join(names)}",
                                **{n: s for n, s in zip(names, shape)})
            return v

        r_ots = sb("r_ots", [P, 2 * S], F32)
        ots = view(r_ots, 0, [2, S])
        wa1s = view(r_ots, 0, [KC, C])
        mrow8 = r_ots[0:1, 1024:1536].bitcast(U8).rearrange("p (b s) -> p b s", b=NB)
        ones = r_ots[0:1, 1536:2048].bitcast(BF16)
        r_attn = sb("r_attn", [P, 4608], F32)
        attn = view(r_attn, 0, [4, S])
        wa2s = view(r_attn, 0, [KC, 6 * C])
        ba2s = view(r_attn, 3072, [6 * C])
        wqkvs = sb("wqkvs", [P, KC, 3 * C], F32)
        wps = sb("wps", [P, KC, C], F32)
        w1s = sb("w1s", [P, KC, FF], F32)
        zeros = w1s[:, 0, 0:BLK // 2].bitcast(BF16)
        w2s = sb("w2s", [P, FF // P, C], F32)
        cTs = sb("cTs", [P, KC, NB], F32)
        b1s = sb("b1s", [P, FF // P], F32)
        ba1s = sb("ba1s", [P, KC], F32)
        bps = sb("bps", [P, C], F32)
        b2s = sb("b2s", [P, C], F32)
        mods = sb("mods", [P, NB, 6, C], F32)
        mrows = mods[0:NB, 0, :, :].rearrange("b m c -> b (m c)")
        mrow = mods[0:NB, 0, :, :]
        sil = sb("sil", [P, 3, KC * NB], F32)
        identf = sb("identf", [P, P], F32)
        identb = sb("identb", [P, P], BF16)
        mask8 = sb("mask8", [P, NB * QT], U8)
        maskc = sb("maskc", [P, NB, QT], F32)
        maskb = sb("maskb", [P, NB, KT], F32)
        mbias = sb("mbias", [1, NB, S], BF16)
        flagf = sb("flagf", [1, 1], F32)
        flag = sb("flag", [1, 1], I32)
        nmax = sb("nmax", [P, 2, 4, QT], F32)
        nmsp = sb("nmsp", [P, 2, 3, 4 * QT], BF16)
        nmrest = sb("nmrest", [P, 2, 4 * QT], F32)
        nmT = sb("nmT", [96, 2, P], BF16)
        nmall = sb("nmall", [P, UNITS, 4 * QT], F32)
        vunit = sb("vunit", [P, KT, 4 * 2 * D], F32)
        PS = ctx.enter_context(nc.psum_tensor("PS", [P, 8, BLK], F32))

        warm = sb("warm", [P, 1], F32)
        stats = sb("stats", [P, 4, 6], F32)
        mv = sb("mv", [P, 2, 4, 2], F32)
        nwt = sb("nwt", [P, 4, 4], F32)

        with ExitStack() as first:
            def sb1(name, shape, dt):
                return first.enter_context(nc.sbuf_tensor(name, shape, dt))

            r_qst = sb1("r_qst", [P, UNITS * 4 * S // 2], F32)
            qst = view(r_qst, 0, [UNITS * 4, S], BF16)
            r_split = sb1("r_split", [P, 7168], F32)
            ksp = view(r_split, 0, [KC, 3, NB * KB], BF16)
            rest = view(r_split, 1536, [2, BLK])
            qsp = view(r_split, 2560, [3, 3, S], BF16)
            numer = view(r_split, 4608, [S])
            recips = view(r_split, 5632, [S])
            denom = view(r_split, 6656, [HC * S // P])
            kst = sb1("kst", [P, H, NB, KB], BF16)
            vaug = sb1("vaug", [P, UNITS, KT, 4, 2 * D], F32)
            r_x = sb1("r_x", [P, KC * T], F32)
            xTs = view(r_x, 0, [KC, T])
            probs = view(r_x, 0, [4, 2, BLK])

        w1p = [sb(f"w1_{n}", [P, KC, FF], F32R) for n in ("high", "low")]
        w2p = [sb(f"w2_{n}", [P, FF // P, C], F32R) for n in ("high", "low")]
        y1 = sb("y1", [P, 4, C], F32)
        x1 = [sb(f"x1_{i}", [P, 4, C], F32) for i in range(2)]
        x1Th = sb("x1T_high", [P, KC, BLK], F32R)
        hidh = sb("hidden_high", [P, FF // P, BLK], F32R)
        xb = [sb(f"x_block{i}", [P, 4, C], F32) for i in range(2)]
        x1Tl = sb("x1T_low", [P, KC, BLK], F32R)
        y2 = sb("y2", [P, 4, C], F32)
        resid = [sb(f"residual{i}", [P, 4, C], F32) for i in range(2)]
        fin1 = sb("result1", [P, 4, C], F32)
        hidl = sb("hidden_low", [P, FF // P, BLK], F32R)
        hid = sb("hidden", [P, 4, BLK], F32)
        fin = [sb("result0", [P, 4, C], F32), fin1]

        w_loaded, x_loaded = [sem(f"w_loaded{i}") for i in range(3)], [sem(f"x_loaded{i}") for i in range(4)]
        mrow_loaded = sem("mrow_loaded")
        mask_loaded, mlp_loaded = sem("mask_loaded"), sem("mlp_loaded")
        ada_loaded, ada2_loaded, ba2_loaded = sem("ada_loaded"), sem("ada2_loaded"), sem("ba2_loaded")
        zeros_set = sem("zeros_set")
        consts = sem("consts")
        rows_dma = sem("rows_dma")
        proj_done, v_done = sem("proj_done"), sem("v_done")
        hi_done = sem("hi_done")
        rest_done, mid_done = sem("rest_done"), sem("mid_done")
        lo_done = sem("lo_done")
        v_evac = sem("v_evac")
        q_dma, k_dma = [sem(f"q_dma{i}") for i in range(4)], [sem(f"k_dma{i}") for i in range(2)]
        ada1_done, ada2_done = sem("ada1_done"), sem("ada2_done")
        sil_exp = sem("sil_exp")
        mods_raw, mods_set = sem("mods_raw"), sem("mods_set")
        mrows_dma, mods_dma = sem("mrows_dma"), sem("mods_dma")
        mx_done, red_done = sem("mx_done"), sem("red_done")
        nm_split, m_dma = sem("nm_split"), sem("m_dma")
        st_done, exp_done = sem("st_done"), sem("exp_done")
        pv_done, ot_evac = sem("pv_done"), sem("ot_evac")
        ot_dma, nd_dma = [sem("ot_dma0"), sem("ot_dma1")], sem("nd_dma")
        den_dma, recip_done, recip_dma = sem("den_dma"), sem("recip_done"), sem("recip_dma")
        attn_ready = sem("attn_ready")
        flag_step = sem("flag_step")
        sp_passed = sem("sp_passed")
        dve_step = sem("dve_step")
        g_x, g_proj, g_hi, g_mid, g_lo, g_kdma = (sem(n) for n in ("g_x", "g_proj", "g_hi", "g_mid", "g_lo", "g_kdma"))
        g_mx, g_red, g_min = (sem(n) for n in ("g_mx", "g_red", "g_min"))
        g_nm, g_nmT, g_nmTe, g_mdma = (sem(n) for n in ("g_nm", "g_nmT", "g_nmTe", "g_mdma"))
        g_rest, g_vm, g_vcol, g_vu, g_zero, g_zdma, g_old = (sem(n) for n in (
            "g_rest", "g_vm", "g_vcol", "g_vu", "g_zero", "g_zdma", "g_old"))
        g_st, g_exp, g_pv, g_add, g_store = (sem(n) for n in ("g_st", "g_exp", "g_pv", "g_add", "g_store"))
        xb_loaded, out_dma = [sem("xb_loaded0"), sem("xb_loaded1")], [sem("out_dma0"), sem("out_dma1")]
        y1_mm, x1T_mm, fc1_mm, fc2_mm = (sem(n) for n in ("y1_mm", "x1T_mm", "fc1_mm", "fc2_mm"))
        y1_set, x1_done, y2_set, fin_done = (sem(n) for n in ("y1_set", "x1_done", "y2_set", "fin_done"))
        w_high, w_split = sem("w_high"), sem("w_split")
        x1Tl_set = sem("x1Tl_set")
        x1T_set, gelu_done = sem("x1T_set"), sem("gelu_done")
        xb_set, resid_set, hidl_set = sem("xb_set"), sem("resid_set"), sem("hidl_set")

        STEPS = UNITS * CHUNKS
        ITEMS = [("q", 0, 0, 0), ("q", 0, 0, 1), ("k", 0), ("k", 1), ("v", 0), ("v", 1), ("q", 0, 1, 0), ("q", 0, 1, 1),
                 ("q", 1, 0, 0), ("q", 1, 0, 1), ("q", 1, 1, 0), ("q", 1, 1, 1)]
        SPLITS = [it for it in ITEMS if it[0] != "v"]
        bank_of = {it: n % 8 for n, it in enumerate(ITEMS)}
        ITEMS_FIRST = 6
        WEIGHTS_AT = 33
        PROJECT_AT = STEPS - 10
        X1T_BANK = ((6, 0), (6, 7))
        N_Q = len(Q_PARTS) * 16
        G_KDMA = 16 * (KC * len(K_PARTS) + NB)

        def parts_of(item):
            if item[0] == "k":
                return ksp[:, item[1]]
            _, b, c, half = item
            return qsp[:, (2 * b + c) % 3, :, half * BLK:(half + 1) * BLK]

        USES = []
        for u in range(UNITS):
            for s_ in range(2 * QT):
                USES.append(("scores", u, s_ // 2, s_ % 2))
                if u and s_ == SPLIT_LAG - 1:
                    USES.append(("transpose", u - 1))
        USES.append(("transpose", UNITS - 1))
        use_of = {use: n for n, use in enumerate(USES)}

        def uses_before(g):
            if g > STEPS - LAST_STEPS:
                return len(USES)
            return min(LEAD_USES + -(-(2 * QT + 1) * g // CHUNKS) + min(g, FASTER), len(USES) - 1)

        def chunk_of(k):
            return k // 4, k % 2, k // 2 % 2

        ORDER = [("item", 8, 0), ("ada1",), ("item", 9, 0), ("item", 10, 2), ("uses", 2), ("item", 11, 3), ("uses", 2),
                 ("ada2", 0, 3), ("uses", 2), ("ada2", 1, 3), ("uses", 2), ("ada2", 2, 3), ("uses", LEAD_USES - 22)]
        ADA2_BANKS = (7, 0, 1)

        def walk(on_item, on_ada1, on_ada2, on_use):
            used = 0
            for what, *arg in ORDER:
                if what == "ada1":
                    on_ada1()
                    continue
                for _ in range(arg[-1]):
                    on_use(used)
                    used += 1
                if what == "item":
                    on_item(arg[0])
                elif what == "ada2":
                    on_ada2(arg[0])

        RECIP_AT = tuple(uses_before(16 * v + 25) for v in range(2))

        def weights(n):
            if n < 4:
                return [w[:, :, 2 * P * n:2 * P * (n + 1)] for w in (w1s, *w1p)]
            return [w[:, 2 * (n - 4):2 * (n - 3), :] for w in (w2s, *w2p)]

        def nothing(*_):
            pass

        block = ctx.enter_context(nc.Block())


        def sp_wait(signal, value):
            nc.sync.wait_ge(signal, value)
            nc.sync.sem_inc(sp_passed, 1)

        def general_sp(sp, xv, k_rows, load_rows):
            xg = xTs[:, :, 0:NB * KB].rearrange("p k (b t) -> p k b t", b=NB)

            def project(k, kb):
                for b in range(NB):
                    sp.dma_start(xg[:, :, b, :], xv[:, :, b, bass.ds(kb * KB, KB)]).then_inc(g_x, 16)
                sp_wait(g_lo, k + 1)
                for c in range(KC):
                    k_rows(c, g_kdma)
                for b in range(NB):
                    sp.dma_start(kst[ONE_ROW:ONE_ROW + 1, :, b, :],
                                 mbias[0:1, b:b + 1, bass.ds(kb * KB, KB)].to_broadcast([1, H, KB])).then_inc(g_kdma, 16)
                sp_wait(g_kdma, G_KDMA * (k + 1))

            with sp.Fori(0, NKB) as kb:
                project(kb, kb)
                sp_wait(g_mx, 2 * QT * UNITS * kb + 2 * QT * UNITS)
            with sp.Fori(0, UNITS) as u:
                sp_wait(g_nmTe, u + 1)
                sp.dma_start(qst[MAX_ROW:ROWS, bass.ds(4 * u, 4), :], nmT[:, 0, :]).then_inc(g_mdma, 16)
                sp_wait(g_mdma, 16 * (u + 1))
            sp.wait_ge(g_zero, 1)
            with sp.Fori(0, UNITS) as u:
                sp.dma_start(ot_dram[bass.ds(u, 1), :, :].rearrange("o p t -> (o p) t"), ots[:, 0, :]).then_inc(g_zdma, 16)
                sp_wait(g_zdma, 16 * (u + 1))
            with sp.Fori(0, NKB) as kb:
                project(kb + NKB, kb)
                with sp.Fori(0, UNITS) as u:
                    row = ot_dram[bass.ds(u, 1), :, :].rearrange("o p t -> (o p) t")
                    sp.dma_start(ots[:, 0, :], row).then_inc(g_old, 16)
                    sp_wait(g_add, 2 * UNITS * kb + 2 * u + 2)
                    sp.dma_start(row, ots[:, 1, :]).then_inc(g_store, 16)
                    sp_wait(g_store, 16 * UNITS * kb + 16 * u + 16)
            with sp.Fori(0, 4) as v:
                load_rows(v, sp_wait)
                sp_wait(attn_ready, v + 1)

        def general_pe(pe, scores, scores_T, with_v):
            def project(k, with_values):
                pe.wait_ge(g_x, 32 * k + 32)
                xg = xTs[:, :, 0:NB * KB]
                for c in range(KC):
                    for kc in range(KC):
                        last = nc.tensor.matmul(PS[:, c, :], wqkvs[:, kc, C + P * c:C + P * (c + 1)], xg[:, kc, :],
                                                start=kc == 0, stop=kc == KC - 1)
                if with_values:
                    for b in range(NB):
                        for kt in range(KT):
                            for kc in range(KC):
                                last = nc.tensor.matmul(PS[:, 2 + b, kt * C:(kt + 1) * C],
                                                        xg[:, kc, KB * b + P * kt:KB * b + P * (kt + 1)],
                                                        wqkvs[:, kc, 2 * C:3 * C], start=kc == 0, stop=kc == KC - 1)
                last.then_inc(g_proj, 1)

            for v in range(4):
                pe.wait_ge(q_dma[v], N_Q)
            pe.wait_ge(red_done, LEAD_USES)
            pe.wait_ge(rest_done, len(SPLITS))
            pe.wait_ge(mods_raw, 3)
            with pe.Fori(0, NKB) as kb:
                project(kb, False)
                for b in range(NB):
                    with pe.Fori(0, 4) as g:
                        n = 2 * QT * UNITS * kb + 2 * QT * 4 * b + 2 * QT * g
                        pe.wait_ge(g_kdma, G_KDMA * kb + G_KDMA)
                        for qt in range(QT):
                            for pr in range(2):
                                if qt >= 1:
                                    pe.wait_ge(g_red, n + 2 * qt + pr - 1)
                                for i in range(2):
                                    last = scores(PS[:, 4 + pr, KB * i:KB * (i + 1)], b, g, 2 * pr + i, qt)
                                last.then_inc(g_mx, 1)
                        pe.wait_ge(g_red, n + 2 * QT)
            with pe.Fori(0, UNITS) as u:
                pe.wait_ge(g_nm, 5 * u + 5)
                nc.tensor.transpose(PS[0:96, 6, 0:P // 2].bitcast(BF16), nmsp[:, 0, :, :].rearrange("p s m -> p (s m)"),
                                    identb[:, :]).then_inc(g_nmT, 1)
            pe.wait_ge(g_mdma, 16 * UNITS)
            with pe.Fori(0, NKB) as kb:
                project(kb + NKB, True)
                for b in range(NB):
                    with pe.Fori(0, 4) as g:
                        u = g + 4 * b
                        n = CHUNKS * UNITS * kb + CHUNKS * u
                        pe.wait_ge(g_kdma, G_KDMA * (kb + NKB) + G_KDMA)
                        pe.wait_ge(g_vm, kb + 1)
                        pe.wait_ge(g_vu, UNITS * kb + u + 1)
                        for k in range(CHUNKS):
                            scores_T(k % 2, b, g, k).then_inc(g_st, 1)
                            pe.wait_ge(g_exp, n + k + 1)
                            with_v(k, lambda kt, h: vunit[:, kt, 32 * h:32 * (h + 1)]).then_inc(g_pv, 1)
                            if k % 4 == 3:
                                pe.wait_ge(g_add, 2 * UNITS * kb + 2 * u + k // 4 + 1)

        def general_dve(dve, split_maxima):
            def parts_of_k(k):
                dve.wait_ge(g_hi, k + 1)
                nc.vector.tensor_tensor(rest[:, :, :], PS[:, 0:2, :], ksp[:, :, 0, :], ALU.subtract).then_inc(g_rest, 1)
                dve.wait_ge(g_rest, k + 1)
                nc.vector.tensor_copy(ksp[:, :, 1, :], rest[:, :, :]).then_inc(g_mid, 1)
                dve.wait_ge(g_mid, k + 1)
                nc.vector.tensor_tensor(ksp[:, :, 2, :], rest[:, :, :], ksp[:, :, 1, :], ALU.subtract).then_inc(g_lo, 1)

            dve.wait_ge(nm_split, 5)
            nc.vector.memset(nmall[:, :, :], 3.0e38).then_inc(g_min, 1)
            with dve.Fori(0, NKB) as kb:
                parts_of_k(kb)
                with dve.Fori(0, UNITS) as u:
                    n = 2 * QT * UNITS * kb + 2 * QT * u
                    dve.wait_ge(g_min, UNITS * kb + u + 1)
                    for qt in range(QT):
                        for pr in range(2):
                            dve.wait_ge(g_mx, n + 2 * qt + pr + 1)
                            nc.vector.tensor_reduce(nmax[:, 0, 2 * pr:2 * pr + 2, qt],
                                                    PS[:, 4 + pr, :].rearrange("p (i t) -> p i t", i=2),
                                                    AX.X, ALU.max, negate=True).then_inc(g_red, 1)
                    dve.wait_ge(g_red, n + 2 * QT)
                    old = nmall[:, bass.ds(u, 1), :].rearrange("p o m -> p (o m)")
                    nc.vector.tensor_tensor(old, old, nmax[:, 0, :, :].rearrange("p i t -> p (i t)"), ALU.min).then_inc(g_min, 1)
            dve.wait_ge(g_min, NKB * UNITS + 1)
            with dve.Fori(0, UNITS) as u:
                split_maxima(dve, nc.vector, nmall[:, bass.ds(u, 1), :].rearrange("p o m -> p (o m)"), 0, g_nm, 5 * u)
                dve.wait_ge(g_nmT, u + 1)
                nc.vector.tensor_copy(nmT[:, 0, :], PS[0:96, 6, 0:P // 2].bitcast(BF16)).then_inc(g_nmTe, 1)
                dve.wait_ge(g_mdma, 16 * u + 16)
            nc.vector.memset(ots[:, 0, :], 0.0).then_inc(g_zero, 1)
            with dve.Fori(0, NKB) as kb:
                parts_of_k(kb + NKB)
                nc.vector.tensor_copy(maskb[:, :, :], maskc[:, :, bass.ds(kb * KT, KT)]).then_inc(g_vcol, 1)
                dve.wait_ge(g_vcol, kb + 1)
                for b in range(NB):
                    for kt in range(KT):
                        nc.vector.tensor_scalar(vaug[:, 4 * b:4 * (b + 1), kt, :, 0:D],
                                                PS[:, 2 + b, C * kt:C * (kt + 1)].rearrange("p (g i d) -> p g i d", i=4, d=D),
                                                maskb[:, b, kt:kt + 1], None, ALU.mult)
                        for g in range(4):
                            last = nc.vector.tensor_copy(vaug[:, 4 * b + g, kt, :, D:2 * D],
                                                         maskb[:, b, kt:kt + 1][:, :, None].to_broadcast([P, 4, D]))
                last.then_inc(g_vm, 1)
                with dve.Fori(0, UNITS) as u:
                    for half in range(2):
                        dve.wait_ge(g_pv, CHUNKS * UNITS * kb + CHUNKS * u + 4 * half + 4)
                        if half == 0:
                            dve.wait_ge(g_old, 16 * UNITS * kb + 16 * u + 16)
                        nc.vector.tensor_tensor(ots[:, 1, BLK * half:BLK * (half + 1)], PS[:, 7, :],
                                                ots[:, 0, BLK * half:BLK * (half + 1)], ALU.add).then_inc(g_add, 1)
        def reciprocal_of(dve, v):
            dve.wait_ge(den_dma, 16 * v + 16)
            nc.vector.reciprocal(denom[:, :], denom[:, :]).then_inc(recip_done, 1)

        def split_maxima(eng, ops, src, at, signal, base):
            rs = nmrest[:, at, :]
            ops.tensor_copy(nmsp[:, at, 0, :], src).then_inc(signal, 1)
            eng.wait_ge(signal, base + 1)
            ops.tensor_tensor(rs, src, nmsp[:, at, 0, :], ALU.subtract).then_inc(signal, 1)
            eng.wait_ge(signal, base + 2)
            ops.tensor_copy(nmsp[:, at, 1, :], rs).then_inc(signal, 1)
            eng.wait_ge(signal, base + 3)
            ops.tensor_tensor(rs, rs, nmsp[:, at, 1, :], ALU.subtract).then_inc(signal, 1)
            eng.wait_ge(signal, base + 4)
            ops.tensor_copy(nmsp[:, at, 2, :], rs).then_inc(signal, 1)

        @block.sync
        def _(sp):
            wv = wqkv.rearrange("(k p) n -> p k n", p=P)
            xv = xT.rearrange("(k p) t -> p k t", p=P)

            def load_w(i):
                sp.dma_start(wqkvs[:, :, C * i:C * (i + 1)], wv[:, :, C * i:C * (i + 1)]).then_inc(w_loaded[i], 16)

            def load_block(i):
                sp.dma_start(xTs[:, :, i * BLK:(i + 1) * BLK], xv[:, :, i * BLK:(i + 1) * BLK]).then_inc(x_loaded[i], 16)

            load_w(0)
            load_block(0)
            load_block(1)
            load_w(1)
            load_block(3)
            load_w(2)
            load_block(2)
            sp.dma_start(mask8[:, :], mask_cols).then_inc(mask_loaded, 16)
            sp.dma_start(identf[:, :], ident).then_inc(mask_loaded, 16)
            sp.wait_ge(consts, 2)
            for b in range(NB):
                sp.dma_start(kst[ONE_ROW:ONE_ROW + 1, :, b, :],
                             mbias[0:1, b:b + 1, S - KB:S].to_broadcast([1, H, KB])).then_inc(rows_dma, 16)
            sp.dma_start(kst[MAX_ROW:ROWS, :, :, :],
                         ones[0:1, None, :].to_broadcast([1, (ROWS - MAX_ROW) * H * NB * KB // S, S])).then_inc(rows_dma, 16)
            sp.dma_start(qst[ONE_ROW:ONE_ROW + 1, :, :],
                         ones[0:1, None, :].to_broadcast([1, UNITS * 4, S])).then_inc(rows_dma, 16)

            sp.dma_start(cTs[:, :, :], cT.rearrange("(k p) b -> p k b", p=P)).then_inc(ada_loaded, 16)
            sp.dma_start(wa1s[:, :, :], wa1.rearrange("(k p) n -> p k n", p=P)).then_inc(ada_loaded, 16)
            sp.dma_start(ba1s[:, :], ba1).then_inc(ada_loaded, 16)

            def stack_q(b, c):
                sp.wait_ge(lo_done, SPLITS.index(("q", b, c, 1)) + 1)
                for n, part in enumerate(Q_PARTS):
                    sp.dma_start(qst[D * n:D * (n + 1), H * b + HC * c:H * b + HC * (c + 1), :],
                                 qsp[:, (2 * b + c) % 3, part, :]).then_inc(q_dma[2 * b + c], 16)

            def k_rows(c, signal):
                for n, part in enumerate(K_PARTS):
                    sp.dma_start(kst[D * n:D * (n + 1), HC * c:HC * (c + 1), :, :],
                                 ksp[:, c, part, :].rearrange("p (b t) -> p b t", b=NB)).then_inc(signal, 16)

            def stack_k(c):
                sp.wait_ge(lo_done, SPLITS.index(("k", c)) + 1)
                k_rows(c, k_dma[c])

            stack_q(0, 0)
            stack_k(0)
            sp.dma_start(wa2s[:, :, :], wa2.rearrange("(k p) n -> p k n", p=P)).then_inc(ada2_loaded, 16)
            stack_q(0, 1)
            stack_k(1)
            sp.dma_start(ba2s[0:NB, :], ba2[None, :].to_broadcast([NB, 6 * C])).then_inc(ba2_loaded, 16)
            stack_q(1, 0)
            stack_q(1, 1)

            def mlp_loads():
                sp.dma_start(wps[:, :, :], wp.rearrange("(k p) n -> p k n", p=P)).then_inc(mlp_loaded, 16)
                sp.dma_start(bps[:, :], bp[None, :].to_broadcast([P, C])).then_inc(mlp_loaded, 16)
                sp.dma_start(w1s[:, :, :], w1.rearrange("(k p) n -> p k n", p=P)).then_inc(mlp_loaded, 16)
                sp.dma_start(b1s[:, :], b1).then_inc(mlp_loaded, 16)
                sp.dma_start(w2s[:, :, :], w2.rearrange("(k p) n -> p k n", p=P)).then_inc(mlp_loaded, 16)
                sp.dma_start(b2s[:, :], b2[None, :].to_broadcast([P, C])).then_inc(mlp_loaded, 16)

            xd = x.rearrange("(t p) c -> p t c", p=P)
            od = out.rearrange("(t p) c -> p t c", p=P)

            def load_x(t):
                sp.dma_start(xb[t % 2][:, :, :], xd[:, 4 * t:4 * t + 4, :]).then_inc(xb_loaded[t % 2], 16)

            def modulation():
                sp.wait_ge(mods_set, 7)
                sp.dma_start(mods_dram, mrows).then_inc(mrows_dma, 16)
                sp.wait_ge(mrows_dma, 16)
                sp.dma_start(mods[:, :, :, :].rearrange("p b m c -> p (b m c)"),
                             mods_dram.rearrange("b n -> (b n)")[None, :].to_broadcast([P, NB * 6 * C])).then_inc(mods_dma, 16)

            def stack_maxima(u):
                sp.wait_ge(red_done, use_of["transpose", u] + 1)
                sp.dma_start(qst[MAX_ROW:ROWS, 4 * u:4 * u + 4, :], nmT[:, u % 2, :]).then_inc(m_dma, 16)

            def rows_out(u):
                sp.wait_ge(ot_evac, 2 * u + 2)
                sp.dma_start(ot_dram[u, :, :], ots[:, u % 2, :]).then_inc(ot_dma[u % 2], 16)

            def load_rows(v, wait=sp.wait_ge):
                rows = ot_dram[bass.ds(2 * v, 2), :, :].rearrange("g (i r) t -> (g i) r t", r=2 * D)
                sp.dma_start(denom[:, :], rows[:, D, :].rearrange("h (s t) -> h s t", t=HC * S // P)).then_inc(den_dma, 16)
                sp.dma_start(numer[:, :], rows[:, 0:D, :]).then_inc(nd_dma, 16)
                wait(recip_done, v + 1)
                back = recip_dram[bass.ds(v, 1), :, :].rearrange("o h t -> (o h) t")
                sp.dma_start(back, denom[:, :]).then_inc(recip_dma, 16)
                wait(recip_dma, 16 * v + 16)
                sp.dma_start(recips[:, :], back[:, None, :].to_broadcast([HC, D, S])).then_inc(nd_dma, 16)

            with nc.sync.register("sp_flag") as r:
                sp.wait_ge(consts, 5)
                sp.reg_load(r, flag[0:1, 0:1])
                with sp.If_eq(r, 0):
                    stack_maxima(0)
                    mlp_loads()
                    stack_maxima(1)
                    for u in range(UNITS):
                        rows_out(u)
                        if u + 2 < UNITS:
                            stack_maxima(u + 2)
                        if u == 0:
                            modulation()
                        if u == 4:
                            load_x(0)
                            load_x(1)
                        if u % 2 == 1:
                            for s_ in ot_dma:
                                sp.wait_ge(s_, 16 * (u // 2 + 1))
                            if u > 1:
                                sp.wait_ge(attn_ready, u // 2)
                            load_rows(u // 2)
                with sp.If_ne(r, 0):
                    mlp_loads()
                    modulation()
                    general_sp(sp, xT.rearrange("(k p) (b t) -> p k b t", p=P, b=NB), k_rows, load_rows)
                    load_x(0)
                    load_x(1)

            for t in range(4):
                if t < 2:
                    sp.wait_ge(x1_done, t + 1)
                    load_x(t + 2)
                if t < 3:
                    sp.wait_ge(fin_done, t + 1)
                    sp.dma_start(od[:, 4 * t:4 * t + 4, :], fin[t % 2][:, :, :]).then_inc(out_dma[t % 2], 16)
            for half in range(2):
                sp.wait_ge(fin_done, half + 4)
                sp.dma_start(od[:, 12 + 2 * half:14 + 2 * half, :],
                             fin[1][:, 2 * half:2 * half + 2, :]).then_inc(out_dma[1], 16)
            sp.wait_ge(out_dma[0], 32)
            sp.wait_ge(out_dma[1], 48)

        @block.gpsimd
        def _(pool):
            def low_weights(n):
                pool.wait_ge(w_high, n + 1)
                w, high, low = weights(n)
                nc.gpsimd.tensor_tensor(low, w, high, ALU.subtract).then_inc(w_split, 1)

            def low_parts(n):
                pool.wait_ge(mid_done, n + 1)
                parts = parts_of(SPLITS[n])
                nc.gpsimd.tensor_tensor(parts[:, 2, :], rest[:, n % 2, :], parts[:, 1, :], ALU.subtract).then_inc(lo_done, 1)

            def add_bias(n):
                pool.wait_ge(ba2_loaded, 16)
                pool.wait_ge(mods_raw, n + 1)
                m = mrows[:, BLK * n:BLK * (n + 1)]
                nc.gpsimd.tensor_tensor(m, m, ba2s[0:NB, BLK * n:BLK * (n + 1)], ALU.add).then_inc(mods_set, 1)

            def split(u):
                at = u % 2
                pool.wait_ge(red_done, use_of["scores", u, QT - 1, 1] + 1)
                if u >= 2:
                    pool.wait_ge(mx_done, use_of["transpose", u - 2] + 1)
                split_maxima(pool, nc.gpsimd, nmax[:, at, :, :].rearrange("p i t -> p (i t)"), at, nm_split, 5 * u)

            for n in range(ITEMS_FIRST):
                low_parts(n)
            walk(lambda n: low_parts(SPLITS.index(ITEMS[n])), nothing, nothing,
                 lambda n: split(0) if USES[n] == ("scores", 0, QT - 1, 1) else None)

            def fold():
                for n in range(3):
                    add_bias(n)
                pool.wait_ge(mods_set, 3)
                for h0 in (0, 3):
                    gate = mrow[:, h0 + 2, :]
                    nc.gpsimd.tensor_tensor(mrow[:, h0, :], mrow[:, h0, :], gate, ALU.mult)
                    nc.gpsimd.tensor_tensor(mrow[:, h0 + 1, :], mrow[:, h0 + 1, :], gate, ALU.mult).then_inc(mods_set, 1)
                pool.wait_ge(mods_set, 5)
                for h0 in (0, 3):
                    nc.gpsimd.tensor_tensor(mrow[:, h0 + 1, :], mrow[:, h0 + 1, :], mrow[:, h0 + 2, :], ALU.add).then_inc(mods_set, 1)

            def normalise(v, n):
                pool.wait_ge(nd_dma, 32 * n)
                nc.gpsimd.tensor_tensor(attn[:, bass.ds(v, 1), :].rearrange("p o t -> p (o t)"),
                                        numer[:, :], recips[:, :], ALU.mult).then_inc(attn_ready, 1)

            def shift_x(t):
                if t == 0:
                    pool.wait_ge(mods_dma, 16)
                pool.wait_ge(xb_loaded[t % 2], 16 * (t // 2 + 1))
                nc.gpsimd.tensor_tensor(xb[t % 2][:, :, :], xb[t % 2][:, :, :],
                                        mods[:, t // 2, 0:1, :].to_broadcast([P, 4, C]), ALU.add).then_inc(xb_set, 1)

            def hidden_low(t, features=range(FF // P)):
                for f in features:
                    n = FF // P * t + f
                    pool.wait_ge(gelu_done, n + 1)
                    nc.gpsimd.tensor_tensor(hidl[:, f, :], hid[:, n % 4, :], hidh[:, f, :], ALU.subtract).then_inc(hidl_set, 1)

            pool.wait_ge(v_evac, NB * KT)
            pool.wait_ge(consts, 5)
            with nc.gpsimd.register("pool_flag") as r:
                pool.reg_load(r, flag[0:1, 0:1])
                with pool.If_eq(r, 0):
                    split(1)
                    fold()
                    split(2)
                    split(3)
                    split(4)
                    normalise(0, 1)
                    split(5)
                    for n in range(3):
                        low_weights(n)
                    split(6)
                    normalise(1, 2)
                    low_weights(3)
                    low_weights(4)
                    split(7)
                    for n in range(5, 8):
                        low_weights(n)
                    shift_x(0)
                    shift_x(1)
                    normalise(2, 3)
                    hidden_low(0, range(0, 6))
                    normalise(3, 4)
                    hidden_low(0, range(6, 8))
                with pool.If_ne(r, 0):
                    fold()
                    with pool.Fori(0, NKB) as kb:
                        with pool.Fori(0, UNITS) as u:
                            pool.wait_ge(g_vm, kb + 1)
                            src = vaug[:, bass.ds(u, 1), :, :, :].rearrange("p o k i d -> p (o k) (i d)")
                            nc.gpsimd.tensor_copy(vunit[:, :, :], src).then_inc(g_vu, 1)
                            pool.wait_ge(g_pv, CHUNKS * UNITS * kb + CHUNKS * u + CHUNKS)
                    with pool.Fori(0, 4) as v:
                        normalise(v, v + 1)
                    for n in range(8):
                        low_weights(n)
                    shift_x(0)
                    shift_x(1)
                    hidden_low(0)

            def residual(t):
                if t == 0:
                    pool.wait_ge(attn_ready, 4)
                if t >= 2:
                    pool.wait_ge(fin_done, t - 1)
                pool.wait_ge(x1_done, t + 1)
                nc.gpsimd.tensor_tensor(resid[t % 2][:, :, :], x1[t % 2][:, :, :],
                                        mods[:, t // 2, 3:4, :].to_broadcast([P, 4, C]), ALU.add).then_inc(resid_set, 1)

            residual(0)
            residual(1)
            for t in range(1, 4):
                if t < 3:
                    shift_x(t + 1)
                hidden_low(t)
                if t < 3:
                    residual(t + 1)

        @block.tensor
        def _(pe):
            keys = xTs[:, :, :].rearrange("p k (b t) -> p k b t", b=NB)[:, :, :, S - KB:S]

            pe.wait_ge(zeros_set, 1)
            for _ in range(WARM_UP):
                nc.tensor.matmul(PS[:, 7, :], zeros[:, 0:P], zeros, start=True, stop=True)

            def item(n, between=nothing):
                it = ITEMS[n]
                pe.wait_ge(w_loaded["qkv".index(it[0])], 16)
                if n >= 8:
                    pe.wait_ge(rest_done, SPLITS.index(ITEMS[n - 8]) + 1)
                bank = PS[:, n % 8, :]
                if it[0] == "v":
                    b = it[1]
                    for kt in range(KT):
                        for k in range(KC):
                            last = nc.tensor.matmul(bank[:, kt * C:(kt + 1) * C], keys[:, k, b, P * kt:P * (kt + 1)],
                                                    wqkvs[:, k, 2 * C:3 * C], start=k == 0, stop=k == KC - 1)
                    last.then_inc(v_done, 1)
                    return
                if it[0] == "q":
                    _, b, c, half = it
                    pe.wait_ge(x_loaded[2 * b + half], 16)
                else:
                    c = it[1]
                    pe.wait_ge(x_loaded[1], 16)
                    pe.wait_ge(x_loaded[3], 16)
                for k in range(KC):
                    if it[0] == "q":
                        last = nc.tensor.matmul(bank, wqkvs[:, k, P * c:P * (c + 1)],
                                                xTs[:, k, b * S + half * BLK:b * S + (half + 1) * BLK],
                                                start=k == 0, stop=k == KC - 1)
                    else:
                        last = nc.tensor.matmul(bank.rearrange("p (b t) -> p b t", b=NB),
                                                wqkvs[:, k, C + P * c:C + P * (c + 1)],
                                                keys[:, k, :, :], start=k == 0, stop=k == KC - 1)
                    if k == 0:
                        between()
                last.then_inc(proj_done, 1)

            def ada1():
                pe.wait_ge(ada_loaded, 16 * 3)
                pe.wait_ge(rest_done, SPLITS.index(ITEMS[7]) + 1)
                for m in range(KC):
                    for k in range(KC):
                        last = nc.tensor.matmul(PS[:, 7, NB * m:NB * (m + 1)], wa1s[:, k, P * m:P * (m + 1)],
                                                cTs[:, k, :], start=k == 0, stop=k == KC - 1)
                last.then_inc(ada1_done, 1)

            def ada2(n, between):
                bank = ADA2_BANKS[n]
                if n == 0:
                    pe.wait_ge(ada2_loaded, 16)
                    pe.wait_ge(dve_step, 4)
                else:
                    pe.wait_ge(rest_done, SPLITS.index(ITEMS[8 + bank]) + 1)
                for k in range(KC):
                    last = nc.tensor.matmul(PS[0:NB, bank, :], sil[:, 2, NB * k:NB * (k + 1)],
                                            wa2s[:, k, BLK * n:BLK * (n + 1)], start=k == 0, stop=k == KC - 1)
                    if k == 0:
                        between()
                last.then_inc(ada2_done, 1)

            def at_head(ap, h):
                return ap[:, bass.ds(h, 1), :].rearrange("p o t -> p (o t)")

            def scores(bank, b, g, i, tile):
                return nc.tensor.matmul(bank, at_head(qst[0:MAX_ROW, :, P * tile:P * (tile + 1)], 16 * b + 4 * g + i),
                                        at_head(kst[0:MAX_ROW, :, b, :], 4 * g + i), start=True, stop=True)

            def scores_T(slot_, b, g, k):
                half, pr, kt = chunk_of(k)
                for i in range(2 * pr, 2 * pr + 2):
                    last = nc.tensor.matmul(PS[:, 2 * slot_ + i % 2, :],
                                            at_head(kst[0:ROWS, :, b, P * kt:P * (kt + 1)], 4 * g + i),
                                            at_head(qst[0:ROWS, :, BLK * half:BLK * (half + 1)], 16 * b + 4 * g + i),
                                            start=True, stop=True)
                return last

            def with_v(k, v_of):
                half, pr, kt = chunk_of(k)
                for i in range(2):
                    h = 2 * pr + i
                    last = nc.tensor.matmul(PS[32 * h:32 * (h + 1), 7, :], v_of(kt, h),
                                            probs[:, k % 4, i, :], start=kt == 0, stop=kt == KT - 1, tile_position=(0, 32 * h))
                return last

            def use(n):
                what, u, *rest_ = USES[n]
                if n == 0:
                    pe.wait_ge(v_evac, NB * KT)
                    pe.wait_ge(rest_done, SPLITS.index(ITEMS[6]) + 1)
                    pe.wait_ge(rows_dma, 64)
                if n >= 3:
                    pe.wait_ge(red_done, n - 2)
                if what == "transpose":
                    pe.wait_ge(nm_split, 5 * u + 5)
                    if u == 0:
                        pe.wait_ge(consts, 4)
                    last = nc.tensor.transpose(PS[0:96, 4 + n % 3, 0:P // 2].bitcast(BF16),
                                               nmsp[:, u % 2, :, :].rearrange("p s m -> p (s m)"), identb[:, :])
                else:
                    qt, pr = rest_
                    if u % 2 == 0 and qt == 0 and pr == 0:
                        pe.wait_ge(q_dma[u // 2], N_Q)
                        if u < 4:
                            pe.wait_ge(k_dma[u // 2], 16 * len(K_PARTS))
                    for i in range(2):
                        last = scores(PS[:, 4 + n % 3, KB * i:KB * (i + 1)], u // 4, u % 4, 2 * pr + i, qt)
                last.then_inc(mx_done, 1)

            def project_tile(t, tile):
                if t == 0 and tile == 0:
                    pe.wait_ge(mlp_loaded, 16 * 6)
                if tile == 0:
                    pe.wait_ge(attn_ready, 2 * (t // 2) + 2)
                if tile % 2 == 0 and t >= 1:
                    pe.wait_ge(y1_set, 2 * t - 1 + tile // 2)
                at = BLK * (t % 2) + P * tile
                for c in range(KC):
                    last = nc.tensor.matmul(PS[:, 4 + tile // 2, C * (tile % 2):C * (tile % 2 + 1)],
                                            attn[:, 2 * (t // 2) + c, at:at + P], wps[:, c, :],
                                            start=c == 0, stop=c == KC - 1)
                if tile % 2:
                    last.then_inc(y1_mm, 1)

            def transpose_x1(t, c):
                pe.wait_ge(x1_done, t + 1)
                if t >= 1:
                    pe.wait_ge(x1Tl_set, 2 * t)
                for tile in range(4):
                    last = nc.tensor.transpose(PS[:, X1T_BANK[min(t, 1)][c], P * tile:P * (tile + 1)],
                                               x1[t % 2][:, tile, P * c:P * (c + 1)], identf[:, :])
                last.then_inc(x1T_mm, 1)

            def products(g):
                u, k = g // CHUNKS, g % CHUNKS
                pe.wait_ge(exp_done, g + 2)
                if g == 0:
                    pe.wait_ge(v_evac, NB * KT)
                    pe.wait_ge(mods_raw, 1)
                if g % 4 == 0 and g:
                    pe.wait_ge(ot_evac, g // 4)
                for k_ in (k, k + 1):
                    last = with_v(k_, lambda kt, h: vaug[:, u, kt, h, :])
                last.then_inc(pv_done, 1)

            def chunk_pair(g):
                u, k = g // CHUNKS, g % CHUNKS
                uses = list(range(uses_before(g), uses_before(g + 2)))
                if g == 0:
                    pe.wait_ge(rest_done, len(SPLITS))
                    pe.wait_ge(mods_raw, 3)
                if k == 0:
                    pe.wait_ge(m_dma, 16 * u + 16)
                for j in range(2):
                    if g:
                        pe.wait_ge(exp_done, g + j - 1)
                    scores_T(j, u // 4, u % 4, k + j).then_inc(st_done, 1)
                    for n in uses[2 * j:2 + j]:
                        use(n)
                if g:
                    products(g - 2)
                for n in uses[3:]:
                    use(n)
                if g == PROJECT_AT:
                    pe.wait_ge(red_done, len(USES))
                    for tile in range(4):
                        project_tile(0, tile)

            for n in range(8):
                item(n)
            used = 0
            for what, *arg in ORDER:
                if what == "ada1":
                    ada1()
                    continue
                run = range(used, used + arg[-1])
                used += arg[-1]

                def uses_between(run=run):
                    for n in run:
                        use(n)

                if what == "item":
                    item(arg[0], uses_between)
                elif what == "ada2":
                    ada2(arg[0], uses_between)
                else:
                    uses_between()
            with nc.tensor.register("pe_flag") as r:
                pe.wait_ge(consts, 5)
                pe.reg_load(r, flag[0:1, 0:1])
                with pe.If_eq(r, 0):
                    for g in range(0, STEPS, 2):
                        chunk_pair(g)
                    transpose_x1(0, 0)
                    products(STEPS - 2)
                    transpose_x1(0, 1)
                with pe.If_ne(r, 0):
                    general_pe(pe, scores, scores_T, with_v)
                    for tile in range(4):
                        project_tile(0, tile)
                    for c in range(KC):
                        transpose_x1(0, c)

            def three_passes(out, a, b, start, stop):
                nc.tensor.matmul(out, a[0], b[0], start=start, stop=False)
                nc.tensor.matmul(out, a[0], b[1], start=False, stop=False)
                return nc.tensor.matmul(out, a[1], b[0], start=False, stop=stop)

            def fc1(t):
                pe.wait_ge(x1Tl_set, 2 * t + 2)
                for f in range(FF // P):
                    n = FF // P * t + f
                    if t == 0:
                        pe.wait_ge(w_split, f // 2 + 1)
                    if n >= 2:
                        pe.wait_ge(gelu_done, n - 1)
                    for c in range(KC):
                        last = three_passes(PS[:, f % 2, :], [w[:, c, P * f:P * (f + 1)] for w in w1p],
                                            (x1Th[:, c, :], x1Tl[:, c, :]), c == 0, c == KC - 1)
                    last.then_inc(fc1_mm, 1)

            def fc2(t):
                for tile in range(4):
                    if tile % 2 == 0 and t >= 1:
                        pe.wait_ge(y2_set, 2 * t - 1 + tile // 2)
                    for f in range(FF // P):
                        if tile == 0:
                            pe.wait_ge(hidl_set, FF // P * t + f + 1)
                        if t == 0 and tile == 0:
                            pe.wait_ge(w_split, 4 + f // 2 + 1)
                        last = three_passes(PS[:, 2 + tile // 2, C * (tile % 2):C * (tile % 2 + 1)],
                                            [h[:, f, P * tile:P * (tile + 1)] for h in (hidh, hidl)],
                                            [w[:, f, :] for w in w2p], f == 0, f == FF // P - 1)
                    if tile % 2:
                        last.then_inc(fc2_mm, 1)

            def project(t):
                for tile in range(4):
                    project_tile(t, tile)

            project_tile(1, 0)
            fc1(0)
            for tile in range(1, 4):
                project_tile(1, tile)
            fc2(0)
            for c in range(KC):
                transpose_x1(1, c)
            project(2)
            for t in range(1, 4):
                fc1(t)
                if t < 3:
                    for c in range(KC):
                        transpose_x1(t + 1, c)
                if t == 1:
                    project(3)
                fc2(t)

        @block.scalar
        def _(act):
            act.dma_start(mrow8[0:1, :, :], mask.rearrange("(o b) s -> o b s", o=1)).then_inc(mrow_loaded, 16)

            def from_bank(n):
                it = ITEMS[n]
                if it[0] == "v":
                    b = it[1]
                    act.wait_ge(v_done, b + 1)
                    act.wait_ge(consts, 3)
                    for kt in range(KT):
                        col = maskc[:, b, QT - KT + kt:QT - KT + kt + 1]
                        nc.scalar.copy(vaug[:, 4 * b:4 * (b + 1), kt, :, D:2 * D],
                                       col[:, :, None, None].to_broadcast([P, 4, 4, D]))
                        nc.scalar.activation(vaug[:, 4 * b:4 * (b + 1), kt, :, 0:D],
                                             PS[:, bank_of[it], C * kt:C * (kt + 1)].rearrange("p (g i d) -> p g i d", i=4, d=D),
                                             ACT.Copy, scale=maskc[:, b, QT - KT + kt:QT - KT + kt + 1]).then_inc(v_evac, 1)
                    return
                act.wait_ge(proj_done, SPLITS.index(it) + 1)
                if it[:3] == ("q", 1, 1):
                    act.wait_ge(q_dma[0], N_Q)
                nc.scalar.copy(parts_of(it)[:, 0, :], PS[:, bank_of[it], :]).then_inc(hi_done, 1)

            def silu_exp():
                act.wait_ge(dve_step, 1)
                nc.scalar.activation(sil[:, 1, :], sil[:, 0, :], ACT.Exp, scale=-1.0).then_inc(sil_exp, 1)

            def ada_out(n):
                act.wait_ge(ada2_done, n + 1)
                nc.scalar.copy(mrows[:, BLK * n:BLK * (n + 1)], PS[0:NB, ADA2_BANKS[n], :]).then_inc(mods_raw, 1)

            from_bank(0)
            for n in range(1, 8):
                from_bank(n)
            walk(from_bank, silu_exp, ada_out, nothing)

            def exps(slot_, k, signal):
                nc.scalar.activation(probs[:, k % 4, :, :], PS[:, 2 * slot_:2 * slot_ + 2, :], ACT.Exp,
                                     scale=float(D) ** -0.5).then_inc(signal, 1)

            def warm_up():
                nc.scalar.activation(warm[:, :], b1s[:, 0:1], ACT.Gelu)

            def high_weights(n):
                if n == 0:
                    act.wait_ge(mlp_loaded, 16 * 6)
                w, high, _ = weights(n)
                nc.scalar.copy(high, w).then_inc(w_high, 1)

            def rows_out(q):
                u, half = q // 2, q % 2
                act.wait_ge(pv_done, 2 * q + 2)
                if half == 0 and u >= 2:
                    act.wait_ge(ot_dma[u % 2], 16 * (u // 2))
                nc.scalar.copy(ots[:, u % 2, BLK * half:BLK * (half + 1)], PS[:, 7, :]).then_inc(ot_evac, 1)

            def x1T_out(t, c):
                act.wait_ge(x1T_mm, 2 * t + c + 1)
                nc.scalar.copy(x1Th[:, c, :], PS[:, X1T_BANK[min(t, 1)][c], :]).then_inc(x1T_set, 1)

            def features(t):
                for f in range(FF // P):
                    n = FF // P * t + f
                    act.wait_ge(fc1_mm, n + 1)
                    if n >= 4:
                        act.wait_ge(hidl_set, n - 3)
                    nc.scalar.activation(hid[:, n % 4, :], PS[:, f % 2, :], ACT.Gelu, bias=b1s[:, f:f + 1])
                    nc.scalar.activation(hidh[:, f, :], PS[:, f % 2, :], ACT.Gelu,
                                         bias=b1s[:, f:f + 1]).then_inc(gelu_done, 1)
                if t < 3:
                    for c in range(KC):
                        x1T_out(t + 1, c)

            with nc.scalar.register("act_flag") as r:
                act.wait_ge(consts, 5)
                act.reg_load(r, flag[0:1, 0:1])
                with act.If_eq(r, 0):
                    for g in range(STEPS):
                        act.wait_ge(st_done, g + 1)
                        if g >= 4:
                            act.wait_ge(pv_done, (g - 4) // 2 + 1)
                        exps(g % 2, g, exp_done)
                        if g % 4 == 1 and g > 1:
                            rows_out(g // 4 - 1)
                        if g % 2 and 0 <= (g - WEIGHTS_AT) // 2 < 8:
                            high_weights((g - WEIGHTS_AT) // 2)
                    x1T_out(0, 0)
                    rows_out(STEPS // 4 - 1)
                    x1T_out(0, 1)
                    warm_up()
                    features(0)
                with act.If_ne(r, 0):
                    def high_parts(k):
                        act.wait_ge(g_proj, k + 1)
                        nc.scalar.copy(ksp[:, :, 0, :], PS[:, 0:2, :]).then_inc(g_hi, 1)

                    with act.Fori(0, NKB) as kb:
                        high_parts(kb)
                    with act.Fori(0, NKB) as kb:
                        high_parts(kb + NKB)
                        with act.Fori(0, UNITS) as u:
                            n = CHUNKS * UNITS * kb + CHUNKS * u
                            for k in range(CHUNKS):
                                act.wait_ge(g_st, n + k + 1)
                                exps(k % 2, k, g_exp)
                                act.wait_ge(g_pv, n + k + 1)
                    for n in range(8):
                        high_weights(n)
                    for c in range(KC):
                        x1T_out(0, c)
                    features(0)

            warm_up()
            for t in range(1, 4):
                features(t)

        @block.vector
        def _(dve):
            steps = [0]

            def step(ins, meanwhile=None):
                steps[0] += 1
                ins.then_inc(dve_step, 1)
                if meanwhile:
                    meanwhile()
                dve.wait_ge(dve_step, steps[0])

            nc.vector.memset(zeros, 0.0).then_inc(zeros_set, 1)
            nc.vector.memset(ones[0:1, :], 1.0).then_inc(consts, 1)
            dve.wait_ge(mrow_loaded, 16)
            nc.vector.tensor_scalar(mbias[0:1, :, :], mrow8[0:1, :, :], MASKED, -MASKED, ALU.mult, ALU.add).then_inc(consts, 1)

            def masks():
                dve.wait_ge(mask_loaded, 32)
                nc.vector.tensor_copy(maskc[:, :, :], mask8[:, :].rearrange("p (b t) -> p b t", b=NB)).then_inc(consts, 1)
                nc.vector.tensor_copy(identb[:, :], identf[:, :]).then_inc(consts, 1)

            def set_flag():
                nc.vector.tensor_reduce(flagf[0:1, :], mrow8[0:1, :, 0:S - KEYS_FAST], AX.XY, ALU.max).then_inc(flag_step, 1)
                dve.wait_ge(flag_step, 1)
                nc.vector.tensor_copy(flag[0:1, :], flagf[0:1, :]).then_inc(consts, 1)

            def rest_of(n):
                it = SPLITS[n]
                parts = parts_of(it)
                dve.wait_ge(hi_done, n + 1)
                if n >= 2:
                    dve.wait_ge(lo_done, n - 1)
                nc.vector.tensor_tensor(rest[:, n % 2, :], PS[:, bank_of[it], :], parts[:, 0, :],
                                        ALU.subtract).then_inc(rest_done, 1)
                dve.wait_ge(rest_done, n + 1)
                nc.vector.tensor_copy(parts[:, 1, :], rest[:, n % 2, :]).then_inc(mid_done, 1)

            def silu():
                dve.wait_ge(ada1_done, 1)
                dve.wait_ge(ada_loaded, 16 * 3)
                step(nc.vector.tensor_tensor(sil[:, 0, :].rearrange("p (k b) -> p k b", b=NB),
                                             PS[:, 7, 0:KC * NB].rearrange("p (k b) -> p k b", b=NB),
                                             ba1s[:, :, None].to_broadcast([P, KC, NB]), ALU.add))
                dve.wait_ge(sil_exp, 1)
                step(nc.vector.tensor_scalar_add(sil[:, 1, :], sil[:, 1, :], 1.0))
                step(nc.vector.reciprocal(sil[:, 1, :], sil[:, 1, :]))
                step(nc.vector.tensor_tensor(sil[:, 2, :], sil[:, 0, :], sil[:, 1, :], ALU.mult))

            def read_use(n):
                what, u, *where = USES[n]
                dve.wait_ge(mx_done, n + 1)
                if what == "transpose":
                    if u >= 2:
                        dve.wait_ge(m_dma, 16 * (u - 1))
                    nc.vector.tensor_copy(nmT[:, u % 2, :], PS[0:96, 4 + n % 3, 0:P // 2].bitcast(BF16)).then_inc(red_done, 1)
                else:
                    qt, pr = where
                    if u >= 2 and qt == 0 and pr == 0:
                        dve.wait_ge(nm_split, 5 * (u - 1))
                    nc.vector.tensor_reduce(nmax[:, u % 2, 2 * pr:2 * pr + 2, qt],
                                            PS[:, 4 + n % 3, :].rearrange("p (i t) -> p i t", i=2),
                                            AX.X, ALU.max, negate=True).then_inc(red_done, 1)

            for n in range(ITEMS_FIRST):
                rest_of(n)
                if n == 1:
                    masks()
                if n == 3:
                    set_flag()
            walk(lambda n: rest_of(SPLITS.index(ITEMS[n])), silu, nothing, read_use)

            def norm(t, half, banks, y, bias, mm, y_set, add, out, done, n, tiles=range(4)):
                if n > 1:
                    dve.wait_ge(done, n - 1)
                part = slice(tiles[0], tiles[-1] + 1)
                for i in range(tiles[0] // 2, tiles[-1] // 2 + 1):
                    dve.wait_ge(mm, 2 * t + i + 1)
                    nc.vector.tensor_tensor(y[:, 2 * i:2 * i + 2, :],
                                            PS[:, banks + i, :].rearrange("p (t c) -> p t c", t=2),
                                            bias[:, None, :].to_broadcast([P, 2, C]), ALU.add).then_inc(y_set, 1)
                dve.wait_ge(y_set, 2 * t + tiles[-1] // 2 + 1)
                for i in tiles:
                    ins = nc.vector.bn_stats(stats[:, i, :], y[:, i, :])
                step(ins)
                for i in tiles:
                    ins = nc.vector.bn_aggr(mv[:, half, i, :], stats[:, i, :])
                step(ins)
                gain = mods[:, t // 2, 3 * half + 1, :]
                var, g, w, a = mv[:, half, part, 1], nwt[:, 0, part], nwt[:, 1, part], nwt[:, 2, part]
                waiting = list(tiles)

                def meanwhile():
                    if waiting:
                        i = waiting.pop(0)
                        nc.vector.scalar_tensor_tensor(y[:, i, :], y[:, i, :], mv[:, half, i, 0:1], gain, ALU.subtract, ALU.mult)

                step(nc.vector.tensor_scalar_add(a, var, EPS), meanwhile)
                nc.vector.tensor_scalar(w, a, -0.5, None, ALU.mult)
                step(nc.vector.tensor_single_scalar(nwt[:, 3, part].bitcast(I32), a.bitcast(I32), 1, ALU.logical_shift_right), meanwhile)
                step(nc.vector.tensor_scalar(g.bitcast(I32), nwt[:, 3, part].bitcast(I32), -1.0, float(0x5F3759DF), ALU.mult, ALU.add), meanwhile)
                for _ in range(3):
                    step(nc.vector.tensor_tensor(a, g, g, ALU.mult), meanwhile)
                    step(nc.vector.tensor_tensor(a, a, w, ALU.mult))
                    step(nc.vector.scalar_tensor_tensor(g, a, 1.5, g, ALU.add, ALU.mult))
                if half == 0:
                    dve.wait_ge(xb_set, t + 1)
                    if t >= 2:
                        dve.wait_ge(resid_set, t - 1)
                else:
                    dve.wait_ge(resid_set, t + 1)
                    if t >= 2:
                        dve.wait_ge(out_dma[t % 2], 16)
                for i in tiles:
                    ins = nc.vector.scalar_tensor_tensor(out[:, i, :], y[:, i, :], nwt[:, 0, i:i + 1], add[:, i, :], ALU.mult, ALU.add)
                ins.then_inc(done, 1)

            def x1T_low(t):
                for c in range(KC):
                    dve.wait_ge(x1T_set, 2 * t + c + 1)
                    nc.vector.tensor_tensor(x1Tl[:, c, :], PS[:, X1T_BANK[min(t, 1)][c], :], x1Th[:, c, :],
                                            ALU.subtract).then_inc(x1Tl_set, 1)

            def norm1(t):
                if t == 0:
                    dve.wait_ge(mlp_loaded, 16 * 6)
                    dve.wait_ge(mods_dma, 16)
                norm(t, 0, 4, y1, bps, y1_mm, y1_set, xb[t % 2], x1[t % 2], x1_done, t + 1)

            def norm2(t, n, tiles=range(4)):
                norm(t, 1, 2, y2, b2s, fc2_mm, y2_set, resid[t % 2], fin[t % 2], fin_done, n, tiles)

            with nc.vector.register("dve_flag") as r:
                dve.wait_ge(consts, 5)
                dve.reg_load(r, flag[0:1, 0:1])
                before = steps[0]
                with dve.If_eq(r, 0):
                    for n in range(LEAD_USES, len(USES)):
                        if n in RECIP_AT:
                            reciprocal_of(dve, RECIP_AT.index(n))
                        read_use(n)
                    reciprocal_of(dve, 2)
                    norm1(0)
                    x1T_low(0)
                    reciprocal_of(dve, 3)
                    norm1(1)
                with dve.If_ne(r, 0):
                    steps[0] = before
                    general_dve(dve, split_maxima)
                    with dve.Fori(0, 4) as v:
                        reciprocal_of(dve, v)
                    norm1(0)
                    x1T_low(0)
                    norm1(1)
            for t in range(3):
                x1T_low(t + 1)
                if t < 2:
                    norm1(t + 2)
                norm2(t, t + 1)
            norm2(3, 4, range(0, 2))
            norm2(3, 5, range(2, 4))

INPUTS = ("xT", "x", "cT", "mask", "mask_cols", "ident", "wqkv", "wp", "bp", "w1", "b1", "w2", "b2", "wa1", "ba1", "wa2", "ba2")


def kernel(x, cond_1024, mask_BxS_bk0, L0_cond_qkv_w, L0_cond_proj_w, L0_cond_proj_b, L0_cond_fc1_w, L0_cond_fc1_b,
           L0_cond_fc2_w, L0_cond_fc2_b, L0_cond_ada1_w, L0_cond_ada1_b, L0_cond_ada2_w, L0_cond_ada2_b):
    import concourse.bacc as bacc
    from concourse.bass_utils import run_bass_kernel_spmd

    tokens = np.asarray(x).reshape(T, C)
    mask = np.asarray(mask_BxS_bk0)
    qkv = np.asarray(L0_cond_qkv_w)
    qk = qkv[:, :2 * C].reshape(C, 2, KC, HC, D).transpose(0, 1, 2, 4, 3).reshape(C, 2 * C)
    arrays = {
        "xT": tokens.T, "x": tokens, "cT": np.asarray(cond_1024).T, "mask": mask,
        "mask_cols": mask.reshape(NB * QT, P).T, "ident": np.eye(P, dtype=np.float32),
        "wqkv": np.concatenate([qk, qkv[:, 2 * C:]], axis=1), "wp": L0_cond_proj_w, "bp": L0_cond_proj_b,
        "w1": L0_cond_fc1_w, "b1": np.asarray(L0_cond_fc1_b).reshape(FF // P, P).T, "w2": L0_cond_fc2_w, "b2": L0_cond_fc2_b,
        "wa1": L0_cond_ada1_w, "ba1": np.asarray(L0_cond_ada1_b).reshape(KC, P).T, "wa2": L0_cond_ada2_w, "ba2": L0_cond_ada2_b,
    }
    arrays = {n: np.ascontiguousarray(a) for n, a in arrays.items()}
    nc = bacc.Bacc("TRN2", target_bir_lowering=False, num_devices=1)
    aps = [nc.dram_tensor(f"in_{n}", arrays[n].shape, mybir.dt.from_np(arrays[n].dtype), kind="ExternalInput").ap()
           for n in INPUTS]
    result = nc.dram_tensor("result", (T, C), F32, kind="ExternalOutput").ap()
    cond_block(nc, *aps, result)
    r = run_bass_kernel_spmd(nc, [{f"in_{n}": a for n, a in arrays.items()}], core_ids=[0])
    return r.results[0]["result"].reshape(NB, S, C)
```
